# Optimizing a Trainium2 kernel written in Bass

```python
import numpy as np
import jax
import jax.numpy as jnp

def _softmax(x, axis=-1):
    return jax.nn.softmax(x, axis=axis)

def _gelu(x):
    return jax.nn.gelu(x, approximate=True)

def _silu(x):
    return jax.nn.silu(x)

def _sigmoid(x):
    return jax.nn.sigmoid(x)

def _layernorm(x, axis=-1, eps=1e-05):
    m = jnp.mean(x, axis=axis, keepdims=True)
    v = jnp.var(x, axis=axis, keepdims=True)
    return (x - m) / jnp.sqrt(v + eps)

def _scatter_add(tgt, idx, src, axis=0):
    return tgt.at[idx].add(src)

def _segment_sum(src, seg, n):
    return jax.ops.segment_sum(src, seg, n)
kernel_name = 'mk_recurrent_d1_jaxref_r8_d03f1b'

def setup_inputs(seed: int=0):
    np.random.seed(seed)
    _w = jnp.asarray

    def _L0_attn_setup():
        import jax, jax.numpy as jnp
        import numpy as np
        B, SQ, H = (2, 256, 256)
        NH = 16
        HN = H // NH
        key = jax.random.key(seed)
        ks = jax.random.split(key, 6)
        query = jax.random.normal(ks[0], (B, SQ, H), dtype=jnp.float32)
        k_in = jax.random.normal(ks[1], (B, SQ, H), dtype=jnp.float32)
        v_in = jax.random.normal(ks[2], (B, SQ, H), dtype=jnp.float32)
        Wqkv = jax.random.normal(ks[3], (3 * H, H), dtype=jnp.float32) * (1.0 / np.sqrt(H))
        Wproj = jax.random.normal(ks[4], (H, H), dtype=jnp.float32) * (1.0 / np.sqrt(H))
        bproj = jnp.zeros((H,), dtype=jnp.float32)
        return {'query': query, 'key': k_in, 'value': v_in, 'Wqkv': Wqkv, 'Wproj': Wproj, 'bproj': bproj}
    _L0_attn_in = _L0_attn_setup()

    def _L0_ffn_setup():
        import jax, jax.numpy as jnp
        import numpy as np
        L, N, E, H, K = (256, 8, 256, 1024, 8)
        key = jax.random.key(seed)
        ks = jax.random.split(key, 6)
        return {'x': jax.random.normal(ks[0], (L, N, E), dtype=jnp.float32), 'proj1': jax.random.normal(ks[1], (H, E), dtype=jnp.float32) * 0.02, 'proj1_bias': jax.random.normal(ks[2], (H,), dtype=jnp.float32) * 0.02, 'proj2': jax.random.normal(ks[3], (E, H), dtype=jnp.float32) * 0.02, 'proj2_bias': jax.random.normal(ks[4], (E,), dtype=jnp.float32) * 0.02, 'gate_w': jax.random.normal(ks[5], (E, K), dtype=jnp.float32)}
    _L0_ffn_in = _L0_ffn_setup()
    _d = {'L0_attn_query': _L0_attn_in['query'], 'L0_attn_key': _L0_attn_in['key'], 'L0_attn_value': _L0_attn_in['value'], 'L0_attn_Wqkv': _L0_attn_in['Wqkv'], 'L0_attn_Wproj': _L0_attn_in['Wproj'], 'L0_attn_bproj': _L0_attn_in['bproj'], 'L0_ffn_proj1': _L0_ffn_in['proj1'], 'L0_ffn_proj1_bias': _L0_ffn_in['proj1_bias'], 'L0_ffn_proj2': _L0_ffn_in['proj2'], 'L0_ffn_proj2_bias': _L0_ffn_in['proj2_bias'], 'L0_ffn_gate_w': _L0_ffn_in['gate_w']}
    _x0 = _d['L0_attn_query']
    _d['L0_attn_query'] = jax.random.normal(jax.random.fold_in(jax.random.key(seed), 1), (4, 256, 256), dtype=_x0.dtype)
    del _x0
    return _d

def reference(L0_attn_query, L0_attn_key, L0_attn_value, L0_attn_Wqkv, L0_attn_Wproj, L0_attn_bproj, L0_ffn_proj1, L0_ffn_proj1_bias, L0_ffn_proj2, L0_ffn_proj2_bias, L0_ffn_gate_w):

    def _L0_attn_ref(query, key, value, Wqkv, Wproj, bproj):
        import jax, jax.numpy as jnp
        import numpy as np
        B, SQ, H = (2, 256, 256)
        NH = 16
        HN = H // NH
        b, sq, h = query.shape
        nh, hn = (NH, HN)
        norm = 1.0 / jnp.sqrt(jnp.asarray(hn, query.dtype))
        x = jnp.transpose(query, (1, 0, 2)).reshape(sq * b, h)
        mixed = x @ Wqkv.T
        mixed = mixed.reshape(sq, b, nh, 3, hn)
        q = mixed[..., 0, :]
        k = mixed[..., 1, :]
        v = mixed[..., 2, :]
        q = q.reshape(sq, b * nh, hn).transpose(1, 0, 2)
        k = k.reshape(sq, b * nh, hn).transpose(1, 0, 2)
        v = v.reshape(sq, b * nh, hn).transpose(1, 0, 2)
        attn = jnp.einsum('gqd,gkd->gqk', q, k) * norm
        attn = jax.nn.softmax(attn, axis=-1)
        ctx = jnp.einsum('gqk,gkd->gqd', attn, v)
        ctx = ctx.reshape(nh, b, sq, hn)
        ctx = jnp.transpose(ctx, (2, 1, 0, 3)).reshape(sq * b, h)
        out = ctx @ Wproj.T + bproj
        out = out.reshape(sq, b, h)
        return jnp.transpose(out, (1, 0, 2))

    def _L0_ffn_ref(x, proj1, proj1_bias, proj2, proj2_bias, gate_w):
        import jax, jax.numpy as jnp
        import numpy as np
        L, N, E, H, K = (256, 8, 256, 1024, 8)
        dst = jnp.argmax(jnp.einsum('lne,ek->lnk', x, gate_w), axis=-1)
        h = jax.nn.gelu(jnp.einsum('lne,he->lnh', x, proj1) + proj1_bias, approximate=False)
        out = jnp.einsum('lnh,eh->lne', h, proj2) + proj2_bias
        del dst
        return out
    x = L0_attn_query
    xn = _layernorm(x, axis=-1)
    s = _L0_attn_ref(xn, L0_attn_key, L0_attn_value, L0_attn_Wqkv, L0_attn_Wproj, L0_attn_bproj)
    g = _silu(_L0_ffn_ref(xn, L0_ffn_proj1, L0_ffn_proj1_bias, L0_ffn_proj2, L0_ffn_proj2_bias, L0_ffn_gate_w))
    x = x + s * g
    return x

_drawn_inputs = setup_inputs


def setup_inputs(seed=0):
    import zlib

    import numpy as np

    out = dict(_drawn_inputs(seed))
    spreads = {'L0_attn_bproj': (0.0, 2.0)}
    factors = {'L0_attn_Wqkv': 6.253,
     'L0_attn_Wproj': 6.218,
     'L0_ffn_proj1': 5.661,
     'L0_ffn_proj1_bias': 8.0,
     'L0_ffn_proj2': 4.859,
     'L0_ffn_proj2_bias': 8.0}
    for name, (base, spread) in spreads.items():
        noise = np.random.default_rng([zlib.crc32(name.encode()), seed]).standard_normal(out[name].shape)
        drawn = base * np.exp(spread * noise) if base else spread * noise
        out[name] = jnp.asarray(drawn.astype(out[name].dtype))
    for name, factor in factors.items():
        out[name] = (out[name] * factor).astype(out[name].dtype)
    return out
```

```python
import concourse.bass as bass
from concourse import mybir
from contextlib import ExitStack

B, SQ, E = 4, 256, 256
NH, HN = 16, 16
F = 1024
P = 128
TOK = B * SQ
TT = TOK // P
HALF = TOK // 2
KC = E // P
FC = F // P
EPS = 1e-5
SCALE = HN ** -0.5
HP = NH // 2
GROUPS = B * 4
STK = 48
STM = STK + 2
VW = HN + 1


def build_order():
    order = [("XT", 0)] + [("QK", 0, i) for i in range(4)] + [("XT", 1)]
    order += [("V", 0, p) for p in range(2)] + [("QK", 1, i) for i in range(4)] + [("V", 1, p) for p in range(2)]
    scores, ffn1 = [("S", n) for n in range(B * HP)], [("F1", n) for n in range(2 * FC)]
    order += ffn1[:3]
    early = 24
    rest = ffn1[3:]
    for n in range(early):
        order.append(scores[n])
        if n % HP == 2 and n > HP:
            order.append(("MT", n // HP - 1))
        if n * len(rest) // early != (n + 1) * len(rest) // early:
            order.append(rest[n * len(rest) // early])
    late = scores[early:]
    parts = [("F2", n) for n in range(16)]
    order += parts[:1]
    parts = parts[1:]
    for g in range(GROUPS):
        order += [("ST", 2 * g), ("ST", 2 * g + 1)]
        if g == 1:
            order.append(("MT", 2))
        order += late[:2]
        late = late[2:]
        if g == 6:
            order.append(("MT", 3))
        if parts and g < 4:
            order += parts[:2]
            parts = parts[2:]
        elif parts:
            order += parts[:1]
            parts = parts[1:]
        if g >= 1:
            order.append(("PV", g - 1))
        if g >= 2:
            order.append(("CT", g - 2))
            order += after_ct(g - 2)
    order += [("PV", GROUPS - 1), ("CT", GROUPS - 2)] + after_ct(GROUPS - 2)
    order += [("CT", GROUPS - 1)] + after_ct(GROUPS - 1)
    return order


def after_ct(g):
    b, j = divmod(g, 4)
    if b == 1:
        return [("BT", 0, j)]
    if b == 3:
        return [("BT", 1, j), ("PJ", j)]
    return []


def layer_kernel(nc, x, wqkv, w1, b1, w2, b2, wp, bp, out):
    f32, f32r = mybir.dt.float32, mybir.dt.float32r
    ALU, ACT, AX = mybir.AluOpType, mybir.ActivationFunctionType, mybir.AxisListType
    order = build_order()

    def steps(*kinds):
        return [s for s in order if s[0] in kinds]

    ctx = ExitStack()
    with ctx:
        def sem(name):
            return ctx.enter_context(nc.semaphore(name))

        slab = 205 * 256
        arena = ctx.enter_context(nc.sbuf_tensor("arena", [P, slab], f32))
        base = nc.sbuf_base - slab * 4
        used = [0]

        def at(name, shape, dtype, where=None):
            size = 4
            for n in shape[1:]:
                size *= n
            if where is None:
                where = used[0]
                used[0] += (size + 31) // 32 * 32
                assert used[0] <= slab * 4, (name, used[0])
            return nc.alloc_sbuf_tensor_at(name, shape, dtype, offset=base + where)

        KB = 1024
        hT_at = used[0]
        hT = at("hT", [P, FC, TOK], f32)
        xs = at("xs", [P, TT, E], f32, hT_at + 8 * KB)
        wqkv_raw = at("wqkv_raw", [P, KC, 3 * E], f32, hT_at + 16 * KB)
        w1_raw = at("w1_raw", [P, KC, F], f32, hT_at + 22 * KB)
        stage_at = used[0]
        stage = at("stage", [P, 2, 4, 2, HALF], f32r)
        PT = at("PT", [P, 4, 2, 2, SQ], f32, stage_at)
        ctxn = at("ctxn", [P, 4, 2, E], f32, stage_at + 16 * KB)
        ctxT = at("ctxT", [P, KC, 4, SQ], f32, stage_at + 24 * KB)
        qs = at("qs", [P, HP, TOK], f32r)
        ks = at("ks", [P, HP, TOK], f32r)
        xTh_at = used[0]
        xTh = at("xTh", [P, KC, TOK], f32r)
        xTl_at = used[0]
        xTl = at("xTl", [P, KC, TOK], f32r)
        xb = at("xb", [P, TT, E], f32, xTh_at)
        fin = at("fin", [P, 2, 2, E], f32, xTl_at)
        bg = at("bg", [P, 2, E], f32, xTl_at + 4 * KB)
        w1h = at("w1h", [P, KC, F], f32r)
        w1l = at("w1l", [P, KC, F], f32r)
        w2s = at("w2s", [P, FC, E], f32)
        wps = at("wps", [P, KC, E], f32)
        wq_at = used[0]
        wqh = at("wqh", [P, KC, 3 * E], f32r)
        wql = at("wql", [P, KC, 3 * E], f32r)
        gate = at("gate", [P, TT, E], f32, wq_at)
        yh = at("yh", [P, 2, E], f32, wq_at + 8 * KB)
        th = at("th", [P, 2, E], f32, wq_at + 10 * KB)
        VA = at("VA", [P, TT, NH, VW], f32)
        ident = at("ident", [P, P], f32)
        ones = at("ones", [2, TOK], f32)
        cd = at("cd", [P, 2, SQ], f32)
        b1s = at("b1s", [P, FC], f32)
        b2s = at("b2s", [P, E], f32)
        b2h = at("b2h", [P, E], f32)
        bps = at("bps", [P, E], f32)
        stats = at("stats", [P, TT, 6], f32)
        mv = at("mv", [P, TT, 2], f32)
        veps = at("veps", [P, TT], f32)
        mhalf = at("mhalf", [P, TT], f32)
        rstd = at("rstd", [P, TT], f32)
        negm = at("negm", [P, B, 2, 2, HP], f32)
        mm = at("mm", [2 * HP * 2, B, 2, P], f32r)
        rc = at("rc", [P, 2, 2, 4], f32)

        SC = ctx.enter_context(nc.psum_tensor("SC", [P, 2, 2, 2, SQ], f32))
        G = ctx.enter_context(nc.psum_tensor("G", [P, 3, HALF], f32))
        T = ctx.enter_context(nc.psum_tensor("T", [P, HALF], f32))
        PV = G[:, 2, 0:SQ]

        x_in = [sem(f"x_in{i}") for i in range(4)]
        wqkv_in, w1_in, w2_in, wp_in, bias_in = (sem(n) for n in ("wqkv_in", "w1_in", "w2_in", "wp_in", "bias_in"))
        x_again = sem("x_again")
        stored = [sem(f"stored{j}") for j in range(4)]
        ident_set, ident_ready, ones_ready, va_ones, mhalf_set = (
            sem(n) for n in ("ident_set", "ident_ready", "ones_ready", "va_ones", "mhalf_set"))
        wqkv_hi, wqkv_lo, w1_hi, w1_lo = (sem(n) for n in ("wqkv_hi", "wqkv_lo", "w1_hi", "w1_lo"))
        stats_done, mv_done, veps_done, rstd_done, xn_done = (
            sem(n) for n in ("stats_done", "mv_done", "veps_done", "rstd_done", "xn_done"))
        xt_made, xt_hi, xt_lo = sem("xt_made"), sem("xt_hi"), sem("xt_lo")
        qk_made, qk_hi, qk_lo = sem("qk_made"), sem("qk_hi"), sem("qk_lo")
        v_made, v_out, f1_made, gelu_done = sem("v_made"), sem("v_out"), sem("f1_made"), sem("gelu_done")
        stacked = [sem(f"stacked{h}") for h in range(2)]
        ones_rows = sem("ones_rows")
        s_made, max_done, st_made, exp_done = sem("s_made"), sem("max_done"), sem("st_made"), sem("exp_done")
        mt_made, m_hi, m_lo = sem("mt_made"), sem("m_hi"), sem("m_lo")
        m_rows = [sem(f"m_rows{b}") for b in range(B)]
        pv_made, cd_out, ct_made, rc_done, norm_done = (
            sem(n) for n in ("pv_made", "cd_out", "ct_made", "rc_done", "norm_done"))
        bt_made, bt_out = sem("bt_made"), sem("bt_out")
        f2_made, b2_half, yh_done, th_done, gate_done, bg_done, xb_done = (
            sem(n) for n in ("f2_made", "b2_half", "yh_done", "th_done", "gate_done", "bg_done", "xb_done"))
        pj_made, gated, fin_done = sem("pj_made"), sem("gated"), sem("fin_done")

        count = {}

        def nth(kind):
            count[kind] = count.get(kind, 0) + 1
            return count[kind]

        g_uses, g_free = [], []
        for s in steps("XT", "QK", "V", "F1"):
            for part in range(2 if s[0] == "XT" else 1):
                g_uses.append((s, part))
                g_free.append(({"XT": xt_lo, "QK": qk_lo, "V": v_out, "F1": gelu_done}[s[0]], nth("G" + s[0])))
        g_bank = {use: n % 3 for n, use in enumerate(g_uses)}
        sc_uses = steps("S", "ST")
        sc_free = [({"S": max_done, "ST": exp_done}[s[0]], s[1] + 1) for s in sc_uses]
        sc_slot = {s: n % 2 for n, s in enumerate(sc_uses)}
        t_uses = steps("MT", "CT", "BT")
        t_free = [({"MT": m_lo, "CT": norm_done, "BT": bt_out}[s[0]], nth("T" + s[0])) for s in t_uses]
        bt_index = {s: n for n, s in enumerate(steps("BT"))}

        def wait_free(eng, uses, free, use, ring):
            n = uses.index(use)
            if n >= ring:
                eng.wait_ge(*free[n - ring])

        block = ctx.enter_context(nc.Block())

        @block.sync
        def _(sp):
            x_t = x.rearrange("(t p) e -> p t e", p=P)
            for i in range(4):
                sp.dma_start(xs[:, 2 * i:2 * i + 2, :], x_t[:, 2 * i:2 * i + 2, :]).then_inc(x_in[i], 16)
            sp.dma_start(w2s[:], w2).then_inc(w2_in, 16)
            sp.dma_start(wps[:], wp).then_inc(wp_in, 16)
            sp.wait_ge(ones_ready, 1)
            for par in range(2):
                sp.dma_start(ks[64 * par + STK:64 * par + STM, :, :].bitcast(f32),
                             ones[0:2, None, :].to_broadcast([2, HP, TOK])).then_inc(ones_rows, 16)
            for h in range(2):
                cols = slice(h * HALF, (h + 1) * HALF)
                for i in range(4):
                    stack, parts = (qs, (0, 0, 1)) if i < 2 else (ks, (0, 1, 0))
                    sp.wait_ge(qk_hi, 4 * h + i + 1)
                    sp.wait_ge(qk_lo, 4 * h + i + 1)
                    for n, part in enumerate(parts):
                        row = 64 * (i % 2) + HN * n
                        sp.dma_start(stack[row:row + HN, :, cols].bitcast(f32),
                                     stage[:, h, i, part, :].bitcast(f32)).then_inc(stacked[h], 16)
            for b in range(B):
                sp.wait_ge(m_hi, b + 1)
                sp.wait_ge(m_lo, b + 1)
                for qt in range(2):
                    for part in range(2):
                        c = b * SQ + qt * P
                        sp.dma_start(qs[STK + part:P:64, :, c:c + P].bitcast(f32),
                                     mm[qt * NH:(qt + 1) * NH, b, part, :].bitcast(f32)).then_inc(m_rows[b], 16)
            sp.wait_ge(f1_made, 2 * FC)
            sp.dma_start(xb[:], x_t).then_inc(x_again, 16)
            for j in range(4):
                sp.wait_ge(fin_done, j + 1)
                sp.dma_start(out.rearrange("(t p) e -> p t e", p=P)[:, 2 * j:2 * j + 2, :],
                             fin[:, j % 2, :, :]).then_inc(stored[j], 16)
            for j in range(4):
                sp.wait_ge(stored[j], 16)

        @block.gpsimd
        def _(pool):
            nc.gpsimd.memset(mhalf[:], -0.5).then_inc(mhalf_set, 1)
            nc.gpsimd.memset(ident[:], 0.0).then_inc(ident_set, 1)
            pool.wait_ge(ident_set, 1)
            nc.gpsimd.affine_select(out=ident[:], in_=ident[:], compare_op=ALU.not_equal, fill=1.0, base=0,
                                    pattern=[[-1, P]], channel_multiplier=1).then_inc(ident_ready, 1)
            nc.gpsimd.memset(ones[:], 1.0).then_inc(ones_ready, 1)
            pool.wait_ge(mhalf_set, 1)
            for h in range(2):
                pool.wait_ge(veps_done, h + 1)
                nc.gpsimd.tensor_tensor(rstd[:, 4 * h:4 * h + 4], veps[:, 4 * h:4 * h + 4],
                                        mhalf[:, 4 * h:4 * h + 4], ALU.pow).then_inc(rstd_done, 1)
            nc.gpsimd.memset(VA[:, :, :, HN:VW], 1.0).then_inc(va_ones, 1)
            for kc in range(KC):
                pool.wait_ge(w1_hi, kc + 1)
                nc.gpsimd.tensor_tensor(w1l[:, kc, :], w1_raw[:, kc, :], w1h[:, kc, :].bitcast(f32),
                                        ALU.subtract).then_inc(w1_lo, 1)
            pool.wait_ge(x_again, 16)
            pool.wait_ge(bias_in, 48)
            for b in range(B):
                pool.wait_ge(gate_done, b + 1)
                if b >= 1:
                    pool.wait_ge(xb_done, b)
                nc.gpsimd.tensor_tensor(bg[:], gate[:, 2 * b:2 * b + 2, :],
                                        bps[:, None, :].to_broadcast([P, 2, E]), ALU.mult).then_inc(bg_done, 1)
                pool.wait_ge(bg_done, b + 1)
                nc.gpsimd.tensor_tensor(xb[:, 2 * b:2 * b + 2, :], xb[:, 2 * b:2 * b + 2, :], bg[:],
                                        ALU.add).then_inc(xb_done, 1)

        @block.scalar
        def _(act):
            act.dma_start(wqkv_raw[:], wqkv).then_inc(wqkv_in, 16)
            act.dma_start(w1_raw[:], w1).then_inc(w1_in, 16)
            act.dma_start(b1s[:], b1).then_inc(bias_in, 16)
            act.dma_start(b2s[:], b2.to_broadcast([P, E])).then_inc(bias_in, 16)
            act.dma_start(bps[:], bp.to_broadcast([P, E])).then_inc(bias_in, 16)
            act.wait_ge(wqkv_in, 16)
            for kc in range(KC):
                nc.scalar.activation(wqh[:, kc, :], wqkv_raw[:, kc, :], ACT.Copy).then_inc(wqkv_hi, 1)
            n_xt = n_qk = n_v = n_f1 = n_mt = n_bt = n_f2 = 0
            for s in order:
                if s[0] == "XT":
                    h = s[1]
                    for kc in range(KC):
                        act.wait_ge(xt_made, n_xt + 1)
                        nc.scalar.activation(xTh[:, kc, h * HALF:(h + 1) * HALF], G[:, g_bank[s, kc], :],
                                             ACT.Copy).then_inc(xt_hi, 1)
                        n_xt += 1
                elif s[0] == "QK":
                    h, i = s[1:]
                    act.wait_ge(qk_made, n_qk + 1)
                    nc.scalar.activation(stage[:, h, i, 0, :], G[:, g_bank[s, 0], :], ACT.Copy,
                                         scale=SCALE if i < 2 else 1.0).then_inc(qk_hi, 1)
                    n_qk += 1
                    if n_qk == 4:
                        act.wait_ge(w1_in, 16)
                        for kc in range(KC):
                            nc.scalar.activation(w1h[:, kc, :], w1_raw[:, kc, :], ACT.Copy).then_inc(w1_hi, 1)
                elif s[0] == "V":
                    h, p = s[1:]
                    act.wait_ge(v_made, n_v + 1)
                    tt = 4 * h + 2 * p
                    nc.scalar.activation(VA[:, tt:tt + 2, :, 0:HN],
                                         G[:, g_bank[s, 0], :].rearrange("p (t n d) -> p t n d", t=2, d=HN),
                                         ACT.Copy).then_inc(v_out, 1)
                    n_v += 1
                elif s[0] == "F1":
                    h, f = divmod(s[1], FC)
                    if n_f1 == 0:
                        act.wait_ge(bias_in, 48)
                        act.wait_ge(w1_lo, 2)
                        act.wait_ge(xn_done, TT)
                    act.wait_ge(f1_made, n_f1 + 1)
                    nc.scalar.activation(hT[:, f, h * HALF:(h + 1) * HALF], G[:, g_bank[s, 0], :], ACT.Gelu,
                                         bias=b1s[:, f:f + 1]).then_inc(gelu_done, 1)
                    n_f1 += 1
                elif s[0] == "MT":
                    act.wait_ge(mt_made, n_mt + 1)
                    nc.scalar.activation(mm[:, s[1], 0, :], T[0:2 * HP * 2, 0:P], ACT.Copy).then_inc(m_hi, 1)
                    n_mt += 1
                elif s[0] == "ST":
                    w = s[1]
                    act.wait_ge(st_made, w + 1)
                    if w < 4:
                        act.wait_ge(stacked[0], 192)
                    if w >= 4:
                        act.wait_ge(pv_made, (w - 4) // 2 + 1)
                    nc.scalar.activation(PT[:, w % 4], SC[:, sc_slot[s]], ACT.Exp).then_inc(exp_done, 1)
                elif s[0] == "F2" and s[1] % 4 == 3:
                    act.wait_ge(yh_done, n_f2 + 1)
                    if n_f2 >= 1:
                        act.wait_ge(gate_done, n_f2)
                    nc.scalar.activation(th[:], yh[:], ACT.Tanh).then_inc(th_done, 1)
                    n_f2 += 1
                elif s[0] == "BT":
                    kc, j = s[1:]
                    act.wait_ge(bt_made, n_bt + 1)
                    nc.scalar.activation(ctxT[:, kc, j, :], T[:, 0:SQ], ACT.Copy).then_inc(bt_out, 1)
                    n_bt += 1

        @block.vector
        def _(dve):
            def norm_stats(h):
                for t in range(4 * h, 4 * h + 4):
                    if t % 2 == 0:
                        dve.wait_ge(x_in[t // 2], 16)
                    nc.vector.bn_stats(stats[:, t, :], xs[:, t, :]).then_inc(stats_done, 1)
                for t in range(4 * h, 4 * h + 4):
                    dve.wait_ge(stats_done, t + 1)
                    nc.vector.bn_aggr(mv[:, t, :], stats[:, t, :]).then_inc(mv_done, 1)
                dve.wait_ge(mv_done, 4 * h + 4)
                nc.vector.tensor_scalar_add(veps[:, 4 * h:4 * h + 4], mv[:, 4 * h:4 * h + 4, 1],
                                            EPS).then_inc(veps_done, 1)

            def norm_apply(h):
                dve.wait_ge(rstd_done, h + 1)
                for t in range(4 * h, 4 * h + 4):
                    nc.vector.tensor_scalar(xs[:, t, :], xs[:, t, :], mv[:, t, 0:1], rstd[:, t:t + 1],
                                            ALU.subtract, ALU.mult).then_inc(xn_done, 1)

            norm_stats(0)
            for kc in range(KC):
                dve.wait_ge(wqkv_hi, kc + 1)
                nc.vector.tensor_tensor(wql[:, kc, :], wqkv_raw[:, kc, :], wqh[:, kc, :].bitcast(f32),
                                        ALU.subtract).then_inc(wqkv_lo, 1)
            norm_apply(0)
            norm_stats(1)
            norm_apply(1)
            n_xt = n_qk = n_mt = n_f2 = 0
            for s in order:
                if s[0] == "XT":
                    h = s[1]
                    for kc in range(KC):
                        dve.wait_ge(xt_hi, n_xt + 1)
                        cols = slice(h * HALF, (h + 1) * HALF)
                        nc.vector.tensor_tensor(xTl[:, kc, cols], G[:, g_bank[s, kc], :],
                                                xTh[:, kc, cols].bitcast(f32), ALU.subtract).then_inc(xt_lo, 1)
                        n_xt += 1
                elif s[0] == "QK":
                    h, i = s[1:]
                    dve.wait_ge(qk_hi, n_qk + 1)
                    nc.vector.scalar_tensor_tensor(stage[:, h, i, 1, :], G[:, g_bank[s, 0], :],
                                                   SCALE if i < 2 else 1.0, stage[:, h, i, 0, :].bitcast(f32),
                                                   ALU.mult, ALU.subtract).then_inc(qk_lo, 1)
                    n_qk += 1
                elif s[0] == "S":
                    b, hp = divmod(s[1], HP)
                    dve.wait_ge(s_made, s[1] + 1)
                    nc.vector.tensor_reduce(negm[:, b, :, :, hp].rearrange("p q a -> p a q"), SC[:, sc_slot[s]], axis=AX.X, op=ALU.max,
                                            negate=True).then_inc(max_done, 1)
                elif s[0] == "MT":
                    dve.wait_ge(m_hi, n_mt + 1)
                    nc.vector.tensor_tensor(mm[:, s[1], 1, :], T[0:2 * HP * 2, 0:P],
                                            mm[:, s[1], 0, :].bitcast(f32), ALU.subtract).then_inc(m_lo, 1)
                    n_mt += 1
                elif s[0] == "PV":
                    g = s[1]
                    dve.wait_ge(pv_made, g + 1)
                    if g >= 2:
                        dve.wait_ge(ct_made, g - 1)
                    nc.vector.tensor_copy(cd[:, g % 2, :], PV).then_inc(cd_out, 1)
                elif s[0] == "CT":
                    g = s[1]
                    b, j = divmod(g, 4)
                    tv = T[:, 0:2 * P].rearrange("p (q m r) -> p q m r", q=2, r=32)
                    dve.wait_ge(ct_made, g + 1)
                    if g >= 2:
                        dve.wait_ge(norm_done, g - 1)
                    if g == 0:
                        dve.wait_ge(stacked[1], 192)
                    nc.vector.reciprocal(rc[:, g % 2], tv[:, :, :, HN]).then_inc(rc_done, 1)
                    dve.wait_ge(rc_done, g + 1)
                    cols = slice(4 * HN * b, 4 * HN * (b + 1))
                    nc.vector.tensor_tensor(ctxn[:, j, :, cols].rearrange("p q (m d) -> p q m d", d=HN),
                                            tv[:, :, :, 0:HN],
                                            rc[:, g % 2, :, :, None].to_broadcast([P, 2, 4, HN]),
                                            ALU.mult).then_inc(norm_done, 1)
                elif s[0] == "F2" and s[1] == 0:
                    dve.wait_ge(bias_in, 48)
                    nc.vector.tensor_scalar(b2h[:], b2s[:], 0.5, None, ALU.mult).then_inc(b2_half, 1)
                    dve.wait_ge(b2_half, 1)
                elif s[0] == "F2" and s[1] % 4 == 3:
                    dve.wait_ge(f2_made, n_f2 + 1)
                    if n_f2 >= 1:
                        dve.wait_ge(gate_done, n_f2)
                    if n_f2 == 0:
                        dve.wait_ge(v_made, 4)
                    nc.vector.scalar_tensor_tensor(yh[:], G[:, n_f2 % 2, :].rearrange("p (t e) -> p t e", t=2), 0.5,
                                                   b2h[:, None, :].to_broadcast([P, 2, E]),
                                                   ALU.mult, ALU.add).then_inc(yh_done, 1)
                    dve.wait_ge(yh_done, n_f2 + 1)
                    dve.wait_ge(th_done, n_f2 + 1)
                    nc.vector.scalar_tensor_tensor(gate[:, 2 * n_f2:2 * n_f2 + 2, :], th[:], 1.0, yh[:],
                                                   ALU.add, ALU.mult).then_inc(gate_done, 1)
                    n_f2 += 1
                elif s[0] == "PJ":
                    j = s[1]
                    dve.wait_ge(pj_made, j + 1)
                    dve.wait_ge(gate_done, j + 1)
                    dve.wait_ge(xb_done, j + 1)
                    if j >= 2:
                        dve.wait_ge(stored[j - 2], 16)
                    dst = fin[:, j % 2, :, :]
                    nc.vector.tensor_tensor(dst, G[:, j % 2, :].rearrange("p (t e) -> p t e", t=2),
                                            gate[:, 2 * j:2 * j + 2, :], ALU.mult).then_inc(gated, 1)
                    dve.wait_ge(gated, j + 1)
                    nc.vector.tensor_tensor(dst, dst, xb[:, 2 * j:2 * j + 2, :], ALU.add).then_inc(fin_done, 1)

        @block.tensor
        def _(pe):
            def product(dst, lhs, rhs, chunks):
                n, last = 0, None
                for kc in range(chunks):
                    for a, b in ((0, 0), (0, 1), (1, 0)):
                        last = nc.tensor.matmul(dst, lhs(kc, a), rhs(kc, b), start=(n == 0), stop=(n == 3 * chunks - 1))
                        n += 1
                return last

            pe.wait_ge(ident_ready, 1)
            n_f2 = 0
            for s in order:
                if s[0] == "XT":
                    h = s[1]
                    pe.wait_ge(xn_done, 4 * h + 4)
                    for kc in range(KC):
                        wait_free(pe, g_uses, g_free, (s, kc), 3)
                        for t in range(4):
                            last = nc.tensor.transpose(G[:, g_bank[s, kc], t * P:(t + 1) * P],
                                                       xs[:, 4 * h + t, kc * P:(kc + 1) * P], ident[:])
                        last.then_inc(xt_made, 1)
                elif s[0] == "QK":
                    h, i = s[1:]
                    pe.wait_ge(xt_lo, 2 * h + 2)
                    pe.wait_ge(wqkv_lo, 2)
                    wait_free(pe, g_uses, g_free, (s, 0), 3)
                    product(G[:, g_bank[s, 0], :],
                            lambda kc, a: (wqh, wql)[a][:, kc, i * P:(i + 1) * P],
                            lambda kc, a: (xTh, xTl)[a][:, kc, h * HALF:(h + 1) * HALF], KC).then_inc(qk_made, 1)
                elif s[0] == "V":
                    h, p = s[1:]
                    wait_free(pe, g_uses, g_free, (s, 0), 3)
                    for t in range(2):
                        c = (4 * h + 2 * p + t) * P
                        last = product(G[:, g_bank[s, 0], t * E:(t + 1) * E],
                                       lambda kc, a: (xTh, xTl)[a][:, kc, c:c + P],
                                       lambda kc, a: (wqh, wql)[a][:, kc, 2 * E:3 * E], KC)
                    last.then_inc(v_made, 1)
                elif s[0] == "F1":
                    h, f = divmod(s[1], FC)
                    pe.wait_ge(w1_lo, 2)
                    wait_free(pe, g_uses, g_free, (s, 0), 3)
                    product(G[:, g_bank[s, 0], :],
                            lambda kc, a: (w1h, w1l)[a][:, kc, f * P:(f + 1) * P],
                            lambda kc, a: (xTh, xTl)[a][:, kc, h * HALF:(h + 1) * HALF], KC).then_inc(f1_made, 1)
                elif s[0] == "S":
                    b, hp = divmod(s[1], HP)
                    if hp == 0:
                        pe.wait_ge(stacked[b // 2], 192)
                    wait_free(pe, sc_uses, sc_free, s, 2)
                    for qt in range(2):
                        for par in range(2):
                            rows = slice(64 * par, 64 * par + STK)
                            c = b * SQ + qt * P
                            last = nc.tensor.matmul(SC[:, sc_slot[s], par, qt, :], qs[rows, hp, c:c + P],
                                                    ks[rows, hp, b * SQ:(b + 1) * SQ], start=True, stop=True)
                    last.then_inc(s_made, 1)
                elif s[0] == "MT":
                    b = s[1]
                    pe.wait_ge(max_done, HP * (b + 1))
                    wait_free(pe, t_uses, t_free, s, 1)
                    nc.tensor.transpose(T[0:2 * HP * 2, 0:P], negm[:, b].rearrange("p q a h -> p (q a h)"),
                                        ident[:]).then_inc(mt_made, 1)
                elif s[0] == "ST":
                    b, hp = divmod(s[1], HP)
                    if hp == 0:
                        pe.wait_ge(m_rows[b], 64)
                        pe.wait_ge(ones_rows, 32)
                    wait_free(pe, sc_uses, sc_free, s, 2)
                    for kt in range(2):
                        for par in range(2):
                            rows = slice(64 * par, 64 * par + STM)
                            c = b * SQ + kt * P
                            last = nc.tensor.matmul(SC[:, sc_slot[s], par, kt, :], ks[rows, hp, c:c + P],
                                                    qs[rows, hp, b * SQ:(b + 1) * SQ], start=True, stop=True)
                    last.then_inc(st_made, 1)
                elif s[0] == "F2":
                    b, part = divmod(s[1], 4)
                    if part == 0:
                        pe.wait_ge(w2_in, 16)
                        if b == 0:
                            pe.wait_ge(gelu_done, 2 * FC)
                        if b >= 2:
                            pe.wait_ge(yh_done, b - 1)
                    t, k0 = part // 2, (part % 2) * (FC // 2)
                    for fc in range(k0, k0 + FC // 2):
                        c = (2 * b + t) * P
                        last = nc.tensor.matmul(G[:, b % 2, t * E:(t + 1) * E], hT[:, fc, c:c + P], w2s[:, fc, :],
                                                start=(fc == 0), stop=(fc == FC - 1))
                    if part == 3:
                        last.then_inc(f2_made, 1)
                elif s[0] == "PV":
                    g = s[1]
                    b, j = divmod(g, 4)
                    pe.wait_ge(exp_done, 2 * g + 2)
                    if g == 0:
                        pe.wait_ge(v_out, 4)
                        pe.wait_ge(va_ones, 1)
                        pe.wait_ge(gelu_done, 2 * FC)
                    if g >= 1:
                        pe.wait_ge(cd_out, g)
                    for kt in range(2):
                        for m in range(4):
                            w = 2 * g + m // 2
                            last = nc.tensor.matmul(PV[32 * m:32 * m + VW, :], VA[:, 2 * b + kt, 4 * j + m, :],
                                                    PT[:, w % 4, m % 2, kt, :], start=(kt == 0), stop=(kt == 1))
                    last.then_inc(pv_made, 1)
                elif s[0] == "CT":
                    g = s[1]
                    pe.wait_ge(cd_out, g + 1)
                    wait_free(pe, t_uses, t_free, s, 1)
                    for qt in range(2):
                        last = nc.tensor.transpose(T[:, qt * P:(qt + 1) * P], cd[:, g % 2, qt * P:(qt + 1) * P], ident[:])
                    last.then_inc(ct_made, 1)
                elif s[0] == "BT":
                    kc, j = s[1:]
                    pe.wait_ge(norm_done, 4 * (2 * kc + 1) + j + 1)
                    wait_free(pe, t_uses, t_free, s, 1)
                    for qt in range(2):
                        last = nc.tensor.transpose(T[:, qt * P:(qt + 1) * P], ctxn[:, j, qt, kc * P:(kc + 1) * P], ident[:])
                    last.then_inc(bt_made, 1)
                elif s[0] == "PJ":
                    j = s[1]
                    pe.wait_ge(bt_out, bt_index[("BT", 1, j)] + 1)
                    pe.wait_ge(wp_in, 16)
                    if j < 2:
                        pe.wait_ge(yh_done, 3 + j)
                    else:
                        pe.wait_ge(gated, j - 1)
                    for qt in range(2):
                        for kc in range(KC):
                            last = nc.tensor.matmul(G[:, j % 2, qt * E:(qt + 1) * E], ctxT[:, kc, j, qt * P:(qt + 1) * P],
                                                    wps[:, kc, :], start=(kc == 0), stop=(kc == KC - 1))
                    last.then_inc(pj_made, 1)


def kernel(**inputs):
    import numpy as np
    import concourse.bacc as bacc
    from concourse.bass_utils import run_bass_kernel_spmd

    a = {n: np.asarray(v) for n, v in inputs.items()}
    x = a["L0_attn_query"].reshape(TOK, E)
    w = a["L0_attn_Wqkv"].reshape(2, 2, 4, 3, HN, E)
    qk = w[:, :, :, 0:2].transpose(3, 1, 4, 2, 0, 5).reshape(2 * E, E)
    v = w[:, :, :, 2].transpose(2, 0, 1, 3, 4).reshape(E, E)

    def chunks(wt):
        return np.ascontiguousarray(wt.reshape(-1, P, wt.shape[1]).transpose(1, 0, 2))

    arrays = {
        "x": x,
        "wqkv": chunks(np.concatenate([qk, v]).T),
        "w1": chunks(a["L0_ffn_proj1"].T),
        "b1": np.ascontiguousarray(a["L0_ffn_proj1_bias"].reshape(FC, P).T),
        "w2": chunks(a["L0_ffn_proj2"].T),
        "b2": a["L0_ffn_proj2_bias"].reshape(1, E),
        "wp": chunks(a["L0_attn_Wproj"].T),
        "bp": a["L0_attn_bproj"].reshape(1, E),
    }
    nc = bacc.Bacc("TRN2", target_bir_lowering=False, num_devices=1)
    f32 = mybir.dt.float32
    args = [nc.dram_tensor(n, v.shape, f32, kind="ExternalInput").ap() for n, v in arrays.items()]
    out = nc.dram_tensor("out", (TOK, E), f32, kind="ExternalOutput").ap()
    layer_kernel(nc, *args, out)
    r = run_bass_kernel_spmd(nc, [arrays], core_ids=[0])
    return r.results[0]["out"].reshape(B, SQ, E)
```

```python
import concourse.bass as bass
from concourse import mybir
from contextlib import ExitStack

B, SQ, E = 4, 256, 256
NH, HN = 16, 16
F = 1024
P = 128
TOK = B * SQ
TT = TOK // P
HALF = TOK // 2
KC = E // P
FC = F // P
EPS = 1e-5
SCALE = HN ** -0.5
HP = NH // 2
GROUPS = B * 4
STK = 48
STM = STK + 2
WARM = 6
SPREAD = 1.0
VW = HN + 1


def build_order():
    order = [("XT", 0)] + [("QK", 0, i) for i in range(4)] + [("XT", 1)] + [("V", 0, p) for p in range(2)]
    fill = [("QK", 1, i) for i in range(4)] + [("V", 1, p) for p in range(2)]
    fill += [("F1", n) for n in range(FC)]
    fill += [("F2", n, part) for n in range(TT // 2) for part in range(4)]
    fill += [("F1", n) for n in range(FC, 2 * FC)]
    cost = {"QK": 1.3, "V": 1.3, "F1": 1.3, "F2": 0.65}
    total = sum(cost[s[0]] for s in fill)
    spent, n = 0.0, 0
    for s in fill:
        order.append(s)
        spent += cost[s[0]]
        while n < B * HP and spent >= (n + SPREAD) * total / (B * HP):
            order.append(("S", n))
            if n % HP == 2 and n > HP:
                order.append(("MT", n // HP - 1))
            n += 1
    order += [("S", m) for m in range(n, B * HP)]
    parts = [("F2", n, part) for n in range(TT // 2, TT) for part in range(4)]
    for g in range(GROUPS):
        order += [("ST", 2 * g)] + parts[:1]
        parts = parts[1:]
        if g == 1:
            order.append(("MT", B - 1))
        if g >= 2:
            order.append(("CT", g - 2))
        if g == GROUPS - 1:
            order.append(("PJ", 0, 0))
        order.append(("ST", 2 * g + 1))
        if g < 2:
            order += parts[:1]
            parts = parts[1:]
        if g >= 1:
            order.append(("PV", g - 1))
        if g >= 6 and (g - 2) // 4 in (1, 3):
            order.append(("BT", (g - 2) // 8, (g - 2) % 4))
    last = GROUPS - 1
    order += [("PJ", 0, 1), ("PV", last), ("CT", last - 1), ("PJ", 1, 0), ("CT", last), ("BT", 1, 2), ("PJ", 1, 1),
              ("BT", 1, 3), ("PJ", 2, 0), ("PJ", 2, 1), ("PJ", 3, 0), ("PJ", 3, 1)]
    return order


def layer_kernel(nc, x, wqkv, w1, b1, w2, b2, wp, bp, out):
    f32, f32r = mybir.dt.float32, mybir.dt.float32r
    ALU, ACT, AX = mybir.AluOpType, mybir.ActivationFunctionType, mybir.AxisListType
    order = build_order()

    def steps(*kinds):
        return [s for s in order if s[0] in kinds]

    ctx = ExitStack()
    with ctx:
        def sem(name):
            return ctx.enter_context(nc.semaphore(name))

        slab = 53184
        arena = ctx.enter_context(nc.sbuf_tensor("arena", [P, slab], f32))
        base = nc.sbuf_base - slab * 4
        used = [0]

        def at(name, shape, dtype, where=None):
            size = 4
            for n in shape[1:]:
                size *= n
            if where is None:
                where = used[0]
                used[0] += (size + 31) // 32 * 32
                assert used[0] <= slab * 4, (name, used[0])
            return nc.alloc_sbuf_tensor_at(name, shape, dtype, offset=base + where)

        KB = 1024
        hT_at = used[0]
        hTh = at("hTh", [P, FC, HALF], f32r)
        hTl_at = used[0]
        hTl = at("hTl", [P, FC, HALF], f32r)
        hG = at("hG", [P, FC, HALF], f32, hTl_at)
        xs = at("xs", [P, TT, E], f32, hT_at)
        w1_raw = at("w1_raw", [P, KC, F], f32, hT_at + 8 * KB)
        wqkv_raw = at("wqkv_raw", [P, KC, 3 * E], f32, hT_at + 16 * KB)
        w2_raw = at("w2_raw", [P, FC, E], f32, hT_at + 24 * KB)
        stage_at = used[0]
        stage = at("stage", [P, 2, 4, 2, HALF], f32r)
        PT = at("PT", [P, 4, 2, 2, SQ], f32, stage_at)
        ctxn = at("ctxn", [P, 4, 2, E], f32, stage_at + 16 * KB)
        ctxT = at("ctxT", [P, KC, 4, SQ], f32, stage_at + 24 * KB)
        qs = at("qs", [P, HP, TOK], f32r)
        ks = at("ks", [P, HP, TOK], f32r)
        xTh_at = used[0]
        xTh = at("xTh", [P, KC, TOK], f32r)
        xTl_at = used[0]
        xTl = at("xTl", [P, KC, TOK], f32r)
        xb = at("xb", [P, TT, E], f32, xTh_at)
        fin = at("fin", [P, 4, E], f32, xTl_at)
        bg = at("bg", [P, 2, E], f32, xTl_at + 4 * KB)
        w1h = at("w1h", [P, KC, F], f32r)
        w1l = at("w1l", [P, KC, F], f32r)
        w2h = at("w2h", [P, FC, E], f32r)
        w2l = at("w2l", [P, FC, E], f32r)
        wps = at("wps", [P, KC, E], f32)
        wq_at = used[0]
        wqh = at("wqh", [P, KC, 3 * E], f32r)
        wql = at("wql", [P, KC, 3 * E], f32r)
        gate = at("gate", [P, TT, E], f32, wq_at)
        yh = at("yh", [P, 2, E], f32, wq_at + 8 * KB)
        th = at("th", [P, 2, E], f32, wq_at + 10 * KB)
        VA = at("VA", [P, TT, NH, VW], f32)
        ident = at("ident", [P, P], f32)
        ones = at("ones", [2, SQ], f32)
        warm = at("warm", [P, HALF // 2], f32, stage_at)
        cd = at("cd", [P, 2, SQ], f32)
        b1s = at("b1s", [P, FC], f32)
        b2s = at("b2s", [P, E], f32)
        bps = at("bps", [P, E], f32)
        stats = at("stats", [P, TT, 6], f32)
        mv = at("mv", [P, TT, 2], f32)
        veps = at("veps", [P, TT], f32)
        mhalf = at("mhalf", [P, TT], f32)
        rstd = at("rstd", [P, TT], f32)
        negm = at("negm", [P, B, 2, 2, HP], f32)
        mm = at("mm", [2 * HP * 2, 2, 2, P], f32r)
        rc = at("rc", [P, 2, 2, 4], f32)

        SC = ctx.enter_context(nc.psum_tensor("SC", [P, 2, 2, 2, SQ], f32))
        G = ctx.enter_context(nc.psum_tensor("G", [P, 3, HALF], f32))
        T = ctx.enter_context(nc.psum_tensor("T", [P, HALF], f32))
        PV = G[:, 2, 0:SQ]

        x_in = [sem(f"x_in{t}") for t in range(TT)]
        wqkv_in, w1_in, w2_in, wp_in, bias_in = (sem(n) for n in ("wqkv_in", "w1_in", "w2_in", "wp_in", "bias_in"))
        x_again = sem("x_again")
        stored = [sem(f"stored{u}") for u in range(TT)]
        ident_set, ident_ready, ones_ready, va_ones, mhalf_set = (
            sem(n) for n in ("ident_set", "ident_ready", "ones_ready", "va_ones", "mhalf_set"))
        wqkv_hi, wqkv_lo, w1_hi, w1_lo, w2_hi, w2_lo = (
            sem(n) for n in ("wqkv_hi", "wqkv_lo", "w1_hi", "w1_lo", "w2_hi", "w2_lo"))
        stats_done, mv_done, veps_done, rstd_done, xn_done = (
            sem(n) for n in ("stats_done", "mv_done", "veps_done", "rstd_done", "xn_done"))
        xt_made, xt_hi, xt_lo = sem("xt_made"), sem("xt_hi"), sem("xt_lo")
        qk_made, qk_hi, qk_lo = sem("qk_made"), sem("qk_hi"), sem("qk_lo")
        v_made, v_out, f1_made, gelu_done = sem("v_made"), sem("v_out"), sem("f1_made"), sem("gelu_done")
        h_hi, h_lo, warm_set = sem("h_hi"), sem("h_lo"), sem("warm_set")
        stacked = [sem(f"stacked{h}") for h in range(2)]
        ones_rows = sem("ones_rows")
        s_made, max_done, st_made, exp_done = sem("s_made"), sem("max_done"), sem("st_made"), sem("exp_done")
        mt_made, m_hi, m_lo = sem("mt_made"), sem("m_hi"), sem("m_lo")
        m_rows = [sem(f"m_rows{b}") for b in range(B)]
        pv_made, cd_out, ct_made, rc_done, norm_done = (
            sem(n) for n in ("pv_made", "cd_out", "ct_made", "rc_done", "norm_done"))
        bt_made, bt_out = sem("bt_made"), sem("bt_out")
        f2_made, b2_half, yh_done, th_done, gate_done, bg_done, xb_done = (
            sem(n) for n in ("f2_made", "b2_half", "yh_done", "th_done", "gate_done", "bg_done", "xb_done"))
        pj_made, gated, fin_done = sem("pj_made"), sem("gated"), sem("fin_done")

        count = {}

        def nth(kind):
            count[kind] = count.get(kind, 0) + 1
            return count[kind]

        g_uses, g_free = [], []
        for s in order:
            if s[0] in ("XT", "QK", "V", "F1") or (s[0] == "F2" and s[1] < TT // 2 and s[2] == 0):
                for part in range(2 if s[0] == "XT" else 1):
                    g_uses.append((s, part))
                    g_free.append(({"XT": xt_lo, "QK": qk_lo, "V": v_out, "F1": gelu_done, "F2": yh_done}[s[0]],
                                   nth("G" + s[0])))
        g_bank = {use: n % 3 for n, use in enumerate(g_uses)}

        def f2_bank(u):
            return g_bank[("F2", u, 0), 0] if u < 4 else 0

        sc_uses = steps("S", "ST")
        sc_free = [({"S": max_done, "ST": exp_done}[s[0]], s[1] + 1) for s in sc_uses]
        sc_slot = {s: n % 2 for n, s in enumerate(sc_uses)}
        aside = {("CT", GROUPS - 1): 0, ("BT", 1, 3): 1}
        t_uses = [s for s in steps("MT", "CT", "BT") if s not in aside]
        t_free = []
        for s in steps("MT", "CT", "BT"):
            free = ({"MT": m_lo, "CT": norm_done, "BT": bt_out}[s[0]], nth("T" + s[0]))
            if s not in aside:
                t_free.append(free)

        def t_bank(s):
            return SC[:, 0, aside[s]].rearrange("p a c -> p (a c)") if s in aside else T

        bt_index = {s: n for n, s in enumerate(steps("BT"))}

        def wait_free(eng, uses, free, use, ring):
            n = uses.index(use)
            if n >= ring:
                eng.wait_ge(*free[n - ring])

        block = ctx.enter_context(nc.Block())

        @block.sync
        def _(sp):
            x_t = x.rearrange("(t p) e -> p t e", p=P)
            for t in range(TT // 2):
                sp.dma_start(xs[:, t, :], x_t[:, t, :]).then_inc(x_in[t], 16)
            sp.dma_start(wqkv_raw[:], wqkv).then_inc(wqkv_in, 16)
            for t in range(TT // 2, TT):
                sp.dma_start(xs[:, t, :], x_t[:, t, :]).then_inc(x_in[t], 16)
            sp.dma_start(w1_raw[:], w1).then_inc(w1_in, 16)
            sp.dma_start(w2_raw[:], w2).then_inc(w2_in, 16)
            sp.dma_start(wps[:], wp).then_inc(wp_in, 16)
            sp.wait_ge(ones_ready, 1)
            for par in range(2):
                sp.dma_start(ks[64 * par + STK:64 * par + STM, :, :].bitcast(f32)
                             .rearrange("p h (b t) -> p (h b) t", t=SQ),
                             ones[0:2, None, :].to_broadcast([2, HP * B, SQ])).then_inc(ones_rows, 16)
            for h in range(2):
                cols = slice(h * HALF, (h + 1) * HALF)
                for i in range(4):
                    stack, parts = (qs, (0, 0, 1)) if i < 2 else (ks, (0, 1, 0))
                    sp.wait_ge(qk_hi, 4 * h + i + 1)
                    sp.wait_ge(qk_lo, 4 * h + i + 1)
                    for n, part in enumerate(parts):
                        row = 64 * (i % 2) + HN * n
                        sp.dma_start(stack[row:row + HN, :, cols].bitcast(f32),
                                     stage[:, h, i, part, :].bitcast(f32)).then_inc(stacked[h], 16)
            for b in range(B):
                sp.wait_ge(m_hi, b + 1)
                sp.wait_ge(m_lo, b + 1)
                for qt in range(2):
                    for part in range(2):
                        c = b * SQ + qt * P
                        sp.dma_start(qs[STK + part:P:64, :, c:c + P].bitcast(f32),
                                     mm[qt * NH:(qt + 1) * NH, b % 2, part, :].bitcast(f32)).then_inc(m_rows[b], 16)
            sp.wait_ge(f1_made, 2 * FC)
            sp.dma_start(xb[:], x_t).then_inc(x_again, 16)
            for u in range(TT):
                sp.wait_ge(fin_done, u + 1)
                sp.dma_start(out.rearrange("(t p) e -> p t e", p=P)[:, u, :],
                             fin[:, u % 4, :]).then_inc(stored[u], 16)
            for u in range(TT):
                sp.wait_ge(stored[u], 16)

        @block.gpsimd
        def _(pool):
            nc.gpsimd.memset(mhalf[:], -0.5).then_inc(mhalf_set, 1)
            nc.gpsimd.memset(ident[:], 0.0).then_inc(ident_set, 1)
            pool.wait_ge(ident_set, 1)
            nc.gpsimd.affine_select(out=ident[:], in_=ident[:], compare_op=ALU.not_equal, fill=1.0, base=0,
                                    pattern=[[-1, P]], channel_multiplier=1).then_inc(ident_ready, 1)
            nc.gpsimd.memset(ones[:], 1.0).then_inc(ones_ready, 1)
            nc.gpsimd.memset(VA[:, :, :, HN:VW], 1.0).then_inc(va_ones, 1)

            def rsqrt(h):
                pool.wait_ge(mhalf_set, 1)
                pool.wait_ge(veps_done, h + 1)
                nc.gpsimd.tensor_tensor(rstd[:, 4 * h:4 * h + 4], veps[:, 4 * h:4 * h + 4],
                                        mhalf[:, 4 * h:4 * h + 4], ALU.pow).then_inc(rstd_done, 1)

            rsqrt(0)
            for kc in range(KC):
                pool.wait_ge(wqkv_hi, kc + 1)
                nc.gpsimd.tensor_tensor(wql[:, kc, :], wqkv_raw[:, kc, :], wqh[:, kc, :].bitcast(f32),
                                        ALU.subtract).then_inc(wqkv_lo, 1)
            rsqrt(1)
            for kc in range(KC):
                pool.wait_ge(w1_hi, kc + 1)
                nc.gpsimd.tensor_tensor(w1l[:, kc, :], w1_raw[:, kc, :], w1h[:, kc, :].bitcast(f32),
                                        ALU.subtract).then_inc(w1_lo, 1)
            for q in range(2):
                pool.wait_ge(w2_hi, q + 1)
                fs = slice(4 * q, 4 * q + 4)
                nc.gpsimd.tensor_tensor(w2l[:, fs, :], w2_raw[:, fs, :], w2h[:, fs, :].bitcast(f32),
                                        ALU.subtract).then_inc(w2_lo, 1)
            for n in range(2 * FC):
                pool.wait_ge(h_hi, n + 1)
                nc.gpsimd.tensor_tensor(hTl[:, n % FC, :], hG[:, n % FC, :], hTh[:, n % FC, :].bitcast(f32),
                                        ALU.subtract).then_inc(h_lo, 1)
            pool.wait_ge(x_again, 16)
            pool.wait_ge(bias_in, 48)
            for u in range(TT):
                pool.wait_ge(gate_done, u + 1)
                if u >= 2:
                    pool.wait_ge(xb_done, u - 1)
                nc.gpsimd.tensor_tensor(bg[:, u % 2, :], gate[:, u, :], bps[:], ALU.mult).then_inc(bg_done, 1)
                pool.wait_ge(bg_done, u + 1)
                nc.gpsimd.tensor_tensor(xb[:, u, :], xb[:, u, :], bg[:, u % 2, :], ALU.add).then_inc(xb_done, 1)

        @block.scalar
        def _(act):
            act.dma_start(b1s[:], b1).then_inc(bias_in, 16)
            act.dma_start(b2s[:], b2.to_broadcast([P, E])).then_inc(bias_in, 16)
            act.dma_start(bps[:], bp.to_broadcast([P, E])).then_inc(bias_in, 16)
            act.wait_ge(warm_set, 1)
            nc.scalar.activation(rc[0:1, 0, 0, 0:1], warm[0:1, 0:1], ACT.Gelu)
            act.wait_ge(wqkv_in, 16)
            for kc in range(KC):
                nc.scalar.activation(wqh[:, kc, :], wqkv_raw[:, kc, :], ACT.Copy).then_inc(wqkv_hi, 1)
            n_xt = n_qk = n_v = n_f1 = n_mt = n_bt = n_f2 = 0
            for s in order:
                if s[0] == "XT":
                    h = s[1]
                    act.wait_ge(xt_made, h + 1)
                    for kc in range(KC):
                        nc.scalar.activation(xTh[:, kc, h * HALF:(h + 1) * HALF], G[:, g_bank[s, kc], :],
                                             ACT.Copy).then_inc(xt_hi, 1)
                elif s[0] == "QK":
                    h, i = s[1:]
                    act.wait_ge(qk_made, n_qk + 1)
                    nc.scalar.activation(stage[:, h, i, 0, :], G[:, g_bank[s, 0], :], ACT.Copy,
                                         scale=SCALE if i < 2 else 1.0).then_inc(qk_hi, 1)
                    n_qk += 1
                    if n_qk == 4:
                        act.wait_ge(w1_in, 16)
                        for kc in range(KC):
                            nc.scalar.activation(w1h[:, kc, :], w1_raw[:, kc, :], ACT.Copy).then_inc(w1_hi, 1)
                elif s[0] == "V":
                    h, p = s[1:]
                    act.wait_ge(v_made, n_v + 1)
                    tt = 4 * h + 2 * p
                    nc.scalar.activation(VA[:, tt:tt + 2, :, 0:HN],
                                         G[:, g_bank[s, 0], :].rearrange("p (t n d) -> p t n d", t=2, d=HN),
                                         ACT.Copy).then_inc(v_out, 1)
                    n_v += 1
                    if n_v == 2:
                        act.wait_ge(w2_in, 16)
                        for q in range(2):
                            fs = slice(4 * q, 4 * q + 4)
                            nc.scalar.activation(w2h[:, fs, :], w2_raw[:, fs, :], ACT.Copy).then_inc(w2_hi, 1)
                elif s[0] == "F1":
                    f = s[1] % FC
                    if n_f1 == 0:
                        act.wait_ge(bias_in, 48)
                        act.wait_ge(xt_made, 2)
                        act.wait_ge(wqkv_lo, 2)
                    if n_f1 == FC // 2:
                        act.wait_ge(w1_lo, 2)
                        act.wait_ge(w2_lo, 2)
                    if n_f1 == FC:
                        act.wait_ge(f2_made, TT // 2)
                    act.wait_ge(f1_made, n_f1 + 1)
                    nc.scalar.activation(hG[:, f, :], G[:, g_bank[s, 0], :], ACT.Gelu,
                                         bias=b1s[:, f:f + 1]).then_inc(gelu_done, 1)
                    n_f1 += 1
                    act.wait_ge(gelu_done, n_f1)
                    nc.scalar.activation(hTh[:, f, :], hG[:, f, :], ACT.Copy).then_inc(h_hi, 1)
                elif s[0] == "MT":
                    if s[1] >= 2:
                        act.wait_ge(m_rows[s[1] - 2], 64)
                    act.wait_ge(mt_made, n_mt + 1)
                    nc.scalar.activation(mm[:, s[1] % 2, 0, :], T[0:2 * HP * 2, 0:P], ACT.Copy).then_inc(m_hi, 1)
                    n_mt += 1
                elif s[0] == "ST":
                    w = s[1]
                    act.wait_ge(st_made, w + 1)
                    if w < 4:
                        act.wait_ge(stacked[0], 192)
                    if w >= 4:
                        act.wait_ge(pv_made, (w - 4) // 2 + 1)
                    nc.scalar.activation(PT[:, w % 4], SC[:, sc_slot[s]], ACT.Exp).then_inc(exp_done, 1)
                elif s[0] == "F2" and s[2] == 3:
                    u = s[1]
                    act.wait_ge(yh_done, u + 1)
                    if u >= 2:
                        act.wait_ge(gate_done, u - 1)
                    nc.scalar.activation(th[:, u % 2, :], yh[:, u % 2, :], ACT.Tanh).then_inc(th_done, 1)
                elif s[0] == "BT":
                    kc, j = s[1:]
                    act.wait_ge(bt_made, n_bt + 1)
                    nc.scalar.activation(ctxT[:, kc, j, :], t_bank(s)[:, 0:SQ], ACT.Copy).then_inc(bt_out, 1)
                    n_bt += 1

        @block.vector
        def _(dve):
            def normalise(h):
                for t in range(4 * h, 4 * h + 4):
                    dve.wait_ge(x_in[t], 16)
                    nc.vector.bn_stats(stats[:, t, :], xs[:, t, :]).then_inc(stats_done, 1)
                for t in range(4 * h, 4 * h + 4):
                    dve.wait_ge(stats_done, t + 1)
                    nc.vector.bn_aggr(mv[:, t, :], stats[:, t, :]).then_inc(mv_done, 1)
                dve.wait_ge(mv_done, 4 * h + 4)
                nc.vector.tensor_scalar_add(veps[:, 4 * h:4 * h + 4], mv[:, 4 * h:4 * h + 4, 1],
                                            EPS).then_inc(veps_done, 1)
                dve.wait_ge(rstd_done, h + 1)
                for t in range(4 * h, 4 * h + 4):
                    nc.vector.tensor_scalar(xs[:, t, :], xs[:, t, :], mv[:, t, 0:1], rstd[:, t:t + 1],
                                            ALU.subtract, ALU.mult).then_inc(xn_done, 1)

            nc.vector.memset(warm[:], 0.0).then_inc(warm_set, 1)
            normalise(0)
            n_xt = n_qk = n_mt = 0
            for s in order:
                if s[0] == "XT":
                    h = s[1]
                    for kc in range(KC):
                        dve.wait_ge(xt_hi, n_xt + 1)
                        cols = slice(h * HALF, (h + 1) * HALF)
                        nc.vector.tensor_tensor(xTl[:, kc, cols], G[:, g_bank[s, kc], :],
                                                xTh[:, kc, cols].bitcast(f32), ALU.subtract).then_inc(xt_lo, 1)
                        n_xt += 1
                    if h == 0:
                        normalise(1)
                elif s[0] == "QK":
                    h, i = s[1:]
                    dve.wait_ge(qk_hi, n_qk + 1)
                    nc.vector.scalar_tensor_tensor(stage[:, h, i, 1, :], G[:, g_bank[s, 0], :],
                                                   SCALE if i < 2 else 1.0, stage[:, h, i, 0, :].bitcast(f32),
                                                   ALU.mult, ALU.subtract).then_inc(qk_lo, 1)
                    n_qk += 1
                elif s[0] == "S":
                    b, hp = divmod(s[1], HP)
                    dve.wait_ge(s_made, s[1] + 1)
                    nc.vector.tensor_reduce(negm[:, b, :, :, hp].rearrange("p q a -> p a q"), SC[:, sc_slot[s]], axis=AX.X, op=ALU.max,
                                            negate=True).then_inc(max_done, 1)
                elif s[0] == "MT":
                    dve.wait_ge(m_hi, n_mt + 1)
                    nc.vector.tensor_tensor(mm[:, s[1] % 2, 1, :], T[0:2 * HP * 2, 0:P],
                                            mm[:, s[1] % 2, 0, :].bitcast(f32), ALU.subtract).then_inc(m_lo, 1)
                    n_mt += 1
                elif s[0] == "PV":
                    g = s[1]
                    dve.wait_ge(pv_made, g + 1)
                    if g >= 2:
                        dve.wait_ge(ct_made, g - 1)
                    nc.vector.tensor_copy(cd[:, g % 2, :], PV).then_inc(cd_out, 1)
                elif s[0] == "CT":
                    g = s[1]
                    b, j = divmod(g, 4)
                    tv = t_bank(s)[:, 0:2 * P].rearrange("p (q m r) -> p q m r", q=2, r=32)
                    dve.wait_ge(ct_made, g + 1)
                    if g >= 2:
                        dve.wait_ge(norm_done, g - 1)
                    if g == 0:
                        dve.wait_ge(stacked[1], 192)
                    nc.vector.reciprocal(rc[:, g % 2], tv[:, :, :, HN]).then_inc(rc_done, 1)
                    dve.wait_ge(rc_done, g + 1)
                    cols = slice(4 * HN * b, 4 * HN * (b + 1))
                    nc.vector.tensor_tensor(ctxn[:, j, :, cols].rearrange("p q (m d) -> p q m d", d=HN),
                                            tv[:, :, :, 0:HN],
                                            rc[:, g % 2, :, :, None].to_broadcast([P, 2, 4, HN]),
                                            ALU.mult).then_inc(norm_done, 1)
                elif s[0] == "F2" and s[2] == 3:
                    u = s[1]
                    if u == 0:
                        dve.wait_ge(bias_in, 48)
                        nc.vector.tensor_scalar(b2s[:], b2s[:], 0.5, None, ALU.mult).then_inc(b2_half, 1)
                        dve.wait_ge(b2_half, 1)
                        dve.wait_ge(v_made, 4)
                    dve.wait_ge(f2_made, u + 1)
                    if u >= 2:
                        dve.wait_ge(gate_done, u - 1)
                    nc.vector.scalar_tensor_tensor(yh[:, u % 2, :], G[:, f2_bank(u), 0:E], 0.5, b2s[:],
                                                   ALU.mult, ALU.add).then_inc(yh_done, 1)
                    dve.wait_ge(yh_done, u + 1)
                    dve.wait_ge(th_done, u + 1)
                    nc.vector.scalar_tensor_tensor(gate[:, u, :], th[:, u % 2, :], 1.0, yh[:, u % 2, :],
                                                   ALU.add, ALU.mult).then_inc(gate_done, 1)
                elif s[0] == "PJ":
                    u = 2 * s[1] + s[2]
                    dve.wait_ge(pj_made, u + 1)
                    dve.wait_ge(xb_done, u + 1)
                    if u >= 4:
                        dve.wait_ge(stored[u - 4], 16)
                    dst = fin[:, u % 4, :]
                    nc.vector.tensor_tensor(dst, G[:, 1 - u % 2, 0:E], gate[:, u, :], ALU.mult).then_inc(gated, 1)
                    dve.wait_ge(gated, u + 1)
                    nc.vector.tensor_tensor(dst, dst, xb[:, u, :], ALU.add).then_inc(fin_done, 1)

        @block.tensor
        def _(pe):
            def product(dst, lhs, rhs, chunks, first=True, last=True, lhs_lo=None, rhs_lo=None):
                todo = [(kc, a, b) for a, b in ((0, 0), (0, 1), (1, 0)) for kc in chunks]
                for n, (kc, a, b) in enumerate(todo):
                    if rhs_lo and (a, b, kc) == (0, 1, chunks[0]):
                        pe.wait_ge(*rhs_lo)
                    if lhs_lo and (a, b, kc) == (1, 0, chunks[0]):
                        pe.wait_ge(*lhs_lo)
                    m = nc.tensor.matmul(dst, lhs(kc, a), rhs(kc, b), start=first and n == 0,
                                         stop=last and n == len(todo) - 1)
                return m

            def wait_t(s):
                if s in aside:
                    pe.wait_ge(exp_done, B * HP)
                else:
                    wait_free(pe, t_uses, t_free, s, 1)

            pe.wait_ge(warm_set, 1)
            for n in range(WARM):
                nc.tensor.matmul(T[:, 0:HALF // 2], warm[:, 0:P], warm[:], start=True, stop=True)
            pe.wait_ge(ident_ready, 1)
            for s in order:
                if s[0] == "XT":
                    h = s[1]
                    for kc in range(KC):
                        wait_free(pe, g_uses, g_free, (s, kc), 3)
                    for t in range(4):
                        pe.wait_ge(xn_done, 4 * h + t + 1)
                        for kc in range(KC):
                            last = nc.tensor.transpose(G[:, g_bank[s, kc], t * P:(t + 1) * P],
                                                       xs[:, 4 * h + t, kc * P:(kc + 1) * P], ident[:])
                    last.then_inc(xt_made, 1)
                elif s[0] == "QK":
                    h, i = s[1:]
                    pe.wait_ge(xt_hi, 2 * h + 2)
                    pe.wait_ge(wqkv_hi, 2)
                    wait_free(pe, g_uses, g_free, (s, 0), 3)
                    product(G[:, g_bank[s, 0], :],
                            lambda kc, a: (wqh, wql)[a][:, kc, i * P:(i + 1) * P],
                            lambda kc, a: (xTh, xTl)[a][:, kc, h * HALF:(h + 1) * HALF], range(KC),
                            lhs_lo=(wqkv_lo, 2), rhs_lo=(xt_lo, 2 * h + 2)).then_inc(qk_made, 1)
                elif s[0] == "V":
                    h, p = s[1:]
                    wait_free(pe, g_uses, g_free, (s, 0), 3)
                    for t in range(2):
                        c = (4 * h + 2 * p + t) * P
                        last = product(G[:, g_bank[s, 0], t * E:(t + 1) * E],
                                       lambda kc, a: (xTh, xTl)[a][:, kc, c:c + P],
                                       lambda kc, a: (wqh, wql)[a][:, kc, 2 * E:3 * E], range(KC))
                    last.then_inc(v_made, 1)
                elif s[0] == "F1":
                    h, f = divmod(s[1], FC)
                    pe.wait_ge(w1_hi, 2)
                    wait_free(pe, g_uses, g_free, (s, 0), 3)
                    product(G[:, g_bank[s, 0], :],
                            lambda kc, a: (w1h, w1l)[a][:, kc, f * P:(f + 1) * P],
                            lambda kc, a: (xTh, xTl)[a][:, kc, h * HALF:(h + 1) * HALF], range(KC),
                            lhs_lo=(w1_lo, 2)).then_inc(f1_made, 1)
                elif s[0] == "S":
                    b, hp = divmod(s[1], HP)
                    if hp == 0:
                        pe.wait_ge(stacked[b // 2], 192)
                    wait_free(pe, sc_uses, sc_free, s, 2)
                    for qt in range(2):
                        for par in range(2):
                            rows = slice(64 * par, 64 * par + STK)
                            c = b * SQ + qt * P
                            last = nc.tensor.matmul(SC[:, sc_slot[s], par, qt, :], qs[rows, hp, c:c + P],
                                                    ks[rows, hp, b * SQ:(b + 1) * SQ], start=True, stop=True)
                    last.then_inc(s_made, 1)
                elif s[0] == "MT":
                    b = s[1]
                    pe.wait_ge(max_done, HP * (b + 1))
                    wait_free(pe, t_uses, t_free, s, 1)
                    nc.tensor.transpose(T[0:2 * HP * 2, 0:P], negm[:, b].rearrange("p q a h -> p (q a h)"),
                                        ident[:]).then_inc(mt_made, 1)
                elif s[0] == "ST":
                    b, hp = divmod(s[1], HP)
                    if hp == 0:
                        pe.wait_ge(m_rows[b], 64)
                        pe.wait_ge(ones_rows, 32)
                    wait_free(pe, sc_uses, sc_free, s, 2)
                    for kt in range(2):
                        for par in range(2):
                            rows = slice(64 * par, 64 * par + STM)
                            c = b * SQ + kt * P
                            last = nc.tensor.matmul(SC[:, sc_slot[s], par, kt, :], ks[rows, hp, c:c + P],
                                                    qs[rows, hp, b * SQ:(b + 1) * SQ], start=True, stop=True)
                    last.then_inc(st_made, 1)
                elif s[0] == "F2":
                    u, part = s[1:]
                    fs = range(2 * part, 2 * part + 2)
                    c = (u % 4) * P
                    pe.wait_ge(h_lo, FC * (u // 4) + fs[-1] + 1)
                    if part == 0:
                        pe.wait_ge(w2_lo, 2)
                        if u < 4:
                            wait_free(pe, g_uses, g_free, (s, 0), 3)
                        else:
                            pe.wait_ge(gelu_done, 2 * FC)
                            pe.wait_ge(yh_done, u)
                    m = product(G[:, f2_bank(u), 0:E],
                                lambda fc, a: (hTh, hTl)[a][:, fc, c:c + P],
                                lambda fc, a: (w2h, w2l)[a][:, fc, :], fs, first=part == 0, last=part == 3)
                    if part == 3:
                        m.then_inc(f2_made, 1)
                elif s[0] == "PV":
                    g = s[1]
                    b, j = divmod(g, 4)
                    pe.wait_ge(exp_done, 2 * g + 2)
                    if g == 0:
                        pe.wait_ge(v_out, 4)
                        pe.wait_ge(va_ones, 1)
                        pe.wait_ge(gelu_done, 2 * FC)
                        pe.wait_ge(yh_done, 4)
                    if g >= 1:
                        pe.wait_ge(cd_out, g)
                    for kt in range(2):
                        for m in range(4):
                            w = 2 * g + m // 2
                            last = nc.tensor.matmul(PV[32 * m:32 * m + VW, :], VA[:, 2 * b + kt, 4 * j + m, :],
                                                    PT[:, w % 4, m % 2, kt, :], start=(kt == 0), stop=(kt == 1))
                    last.then_inc(pv_made, 1)
                elif s[0] == "CT":
                    g = s[1]
                    pe.wait_ge(cd_out, g + 1)
                    wait_t(s)
                    for qt in range(2):
                        last = nc.tensor.transpose(t_bank(s)[:, qt * P:(qt + 1) * P], cd[:, g % 2, qt * P:(qt + 1) * P], ident[:])
                    last.then_inc(ct_made, 1)
                elif s[0] == "BT":
                    kc, j = s[1:]
                    pe.wait_ge(norm_done, 4 * (2 * kc + 1) + j + 1)
                    wait_t(s)
                    for qt in range(2):
                        last = nc.tensor.transpose(t_bank(s)[:, qt * P:(qt + 1) * P], ctxn[:, j, qt, kc * P:(kc + 1) * P], ident[:])
                    last.then_inc(bt_made, 1)
                elif s[0] == "PJ":
                    j, qt = s[1:]
                    u = 2 * j + qt
                    pe.wait_ge(bt_out, bt_index[("BT", 1, j)] + 1)
                    pe.wait_ge(wp_in, 16)
                    if u < 2:
                        pe.wait_ge(yh_done, TT)
                    else:
                        pe.wait_ge(gated, u - 1)
                    for kc in range(KC):
                        last = nc.tensor.matmul(G[:, 1 - qt, 0:E], ctxT[:, kc, j, qt * P:(qt + 1) * P],
                                                wps[:, kc, :], start=(kc == 0), stop=(kc == KC - 1))
                    last.then_inc(pj_made, 1)


def kernel(**inputs):
    import numpy as np
    import concourse.bacc as bacc
    from concourse.bass_utils import run_bass_kernel_spmd

    a = {n: np.asarray(v) for n, v in inputs.items()}
    x = a["L0_attn_query"].reshape(TOK, E)
    w = a["L0_attn_Wqkv"].reshape(2, 2, 4, 3, HN, E)
    qk = w[:, :, :, 0:2].transpose(3, 1, 4, 2, 0, 5).reshape(2 * E, E)
    v = w[:, :, :, 2].transpose(2, 0, 1, 3, 4).reshape(E, E)

    def chunks(wt):
        return np.ascontiguousarray(wt.reshape(-1, P, wt.shape[1]).transpose(1, 0, 2))

    arrays = {
        "x": x,
        "wqkv": chunks(np.concatenate([qk, v]).T),
        "w1": chunks(a["L0_ffn_proj1"].T),
        "b1": np.ascontiguousarray(a["L0_ffn_proj1_bias"].reshape(FC, P).T),
        "w2": chunks(a["L0_ffn_proj2"].T),
        "b2": a["L0_ffn_proj2_bias"].reshape(1, E),
        "wp": chunks(a["L0_attn_Wproj"].T),
        "bp": a["L0_attn_bproj"].reshape(1, E),
    }
    nc = bacc.Bacc("TRN2", target_bir_lowering=False, num_devices=1)
    f32 = mybir.dt.float32
    args = [nc.dram_tensor(n, v.shape, f32, kind="ExternalInput").ap() for n, v in arrays.items()]
    out = nc.dram_tensor("out", (TOK, E), f32, kind="ExternalOutput").ap()
    layer_kernel(nc, *args, out)
    r = run_bass_kernel_spmd(nc, [arrays], core_ids=[0])
    return r.results[0]["out"].reshape(B, SQ, E)
```

```python
import concourse.bass as bass
from concourse import mybir
from contextlib import ExitStack

B, SQ, E = 4, 256, 256
NH, HN = 16, 16
F = 1024
P = 128
TOK = B * SQ
TT = TOK // P
HALF = TOK // 2
KC = E // P
FC = F // P
EPS = 1e-5
SCALE = HN ** -0.5
HP = NH // 2
GROUPS = B * 4
STK = 48
STM = STK + 2
WARM = 5
VW = HN + 1
LEAD = 3.4
FILL = ("", "ff", "f", "", "f", "", "f", "", "f", "f", "f", "f", "p", "p", "p", "p",
        "f", "f", "f", "f", "p", "g", "p", "", "p", "", "p", "", "p", "", "p", "")


def build_order():
    order = [("XT", 0), ("XT", 1)] + [("QK", 0, i) for i in range(4)]
    order += [("XT", 2), ("XT", 3)] + [("V", 0, p) for p in range(2)]
    order += [("QK", 1, 0), ("QK", 1, 1)]
    between = [("QK", 1, 2), ("QK", 1, 3)] + [("V", 1, p) for p in range(2)]
    between += [("F1", n) for n in range(FC)]
    between += [("F2", n, part) for n in range(TT // 2) for part in range(4)]
    between += [("F1", n) for n in range(FC, 2 * FC)]
    cost = {"QK": 1.3, "V": 1.3, "F1": 1.3, "F2": 0.65}
    total = sum(cost[s[0]] for s in between)
    spent, n = 0.0, 0
    for s in between:
        order.append(s)
        spent += cost[s[0]]
        while n < B * HP and spent >= LEAD + n * (total - LEAD) / (B * HP - 1):
            order.append(("S", n))
            if n % HP == 2 and n > HP:
                order.append(("MT", n // HP - 1))
            n += 1
    late = [("S", m) for m in range(n, B * HP)]
    ffn = [("F2", n, part) for n in range(TT // 2, TT) for part in range(4)]
    projection = [("PJ", u, kc) for u in range(TT) for kc in range(KC)]
    for n in range(3):
        order += late[n:n + 1] + ffn[n:n + 1]
    order += late[3:]
    ffn = ffn[3:]
    for g in range(GROUPS):
        for half in range(2):
            order.append(("ST", 2 * g + half))
            for kind in FILL[2 * g + half]:
                order.append(ffn.pop(0) if kind == "f" else projection.pop(0) if kind == "p" else ("GATE",))
            if half == 0 and g == 0:
                order.append(("MT", B - 1))
            if half == 0 and g >= 2:
                order.append(("CT", g - 2))
        if g >= 1:
            order.append(("PV", g - 1))
        if g >= 3 and g % 2 == 1:
            order.append(("BT", (g - 2) % 4 // 2, (g - 2) // 4))
    assert not ffn and projection[0] == ("PJ", 5, 0)
    last = GROUPS - 1
    return order + [("PV", last), ("CT", last - 1), ("PJ", 5, 0), ("CT", last), ("PJ", 5, 1), ("PJ", 6, 0),
                    ("BT", 1, 3), ("PJ", 7, 0), ("PJ", 6, 1), ("PJ", 7, 1)]


def layer_kernel(nc, x, wqkv, w1, b1, w2, b2, wp, bp, out):
    f32, f32r = mybir.dt.float32, mybir.dt.float32r
    ALU, ACT, AX = mybir.AluOpType, mybir.ActivationFunctionType, mybir.AxisListType
    order = build_order()

    def steps(*kinds):
        return [s for s in order if s[0] in kinds]

    ctx = ExitStack()
    with ctx:
        def sem(name):
            return ctx.enter_context(nc.semaphore(name))

        slab = 53184
        arena = ctx.enter_context(nc.sbuf_tensor("arena", [P, slab], f32))
        base = nc.sbuf_base - slab * 4
        used = [0]

        def at(name, shape, dtype, where=None):
            size = 4
            for n in shape[1:]:
                size *= n
            if where is None:
                where = used[0]
                used[0] += (size + 31) // 32 * 32
                assert used[0] <= slab * 4, (name, used[0])
            return nc.alloc_sbuf_tensor_at(name, shape, dtype, offset=base + where)

        KB = 1024
        hT_at = used[0]
        hTh = at("hTh", [P, FC, HALF], f32r)
        hTl_at = used[0]
        hTl = at("hTl", [P, FC, HALF], f32r)
        hG = at("hG", [P, FC, HALF], f32, hTl_at)
        xs = at("xs", [P, TT, E], f32, hT_at)
        w1_raw = at("w1_raw", [P, KC, F], f32, hT_at + 8 * KB)
        wqkv_raw = at("wqkv_raw", [P, 3, KC, E], f32, hT_at + 16 * KB)
        w2_raw = at("w2_raw", [P, FC, E], f32, hT_at + 24 * KB)
        stage_at = used[0]
        stage = at("stage", [P, 2, 4, 2, HALF], f32r)
        PT = at("PT", [P, 4, 2, 2, SQ], f32, stage_at)
        ctxn = at("ctxn", [P, 2, 2, E], f32, stage_at + 16 * KB)
        wph = at("wph", [P, KC, E], f32r, stage_at + 20 * KB)
        wpl = at("wpl", [P, KC, E], f32r, stage_at + 22 * KB)
        cTh = at("cTh", [P, 2, KC, SQ], f32r, stage_at + 24 * KB)
        cTl = at("cTl", [P, 2, KC, SQ], f32r, stage_at + 28 * KB)
        qs = at("qs", [P, HP, TOK], f32r)
        ks = at("ks", [P, HP, TOK], f32r)
        xTh_at = used[0]
        xTh = at("xTh", [P, KC, TOK], f32r)
        xTl_at = used[0]
        xTl = at("xTl", [P, KC, TOK], f32r)
        xb = at("xb", [P, TT, E], f32, xTh_at)
        fin = at("fin", [P, 4, E], f32, xTl_at)
        bg = at("bg", [P, 2, E], f32, xTl_at + 4 * KB)
        w1h = at("w1h", [P, KC, F], f32r)
        w1l = at("w1l", [P, KC, F], f32r)
        w2h = at("w2h", [P, FC, E], f32r)
        w2l = at("w2l", [P, FC, E], f32r)
        wps = at("wps", [P, KC, E], f32)
        wq_at = used[0]
        wqh = at("wqh", [P, 3, KC, E], f32r)
        wql = at("wql", [P, 3, KC, E], f32r)
        gate = at("gate", [P, TT, E], f32, wq_at)
        yh = at("yh", [P, 2, E], f32, wq_at + 8 * KB)
        th = at("th", [P, 2, E], f32, wq_at + 10 * KB)
        VA = at("VA", [P, TT, NH, VW], f32)
        ident = at("ident", [P, P], f32)
        ones = at("ones", [2, SQ], f32)
        warm = at("warm", [P, HALF // 2], f32, stage_at)
        cd = at("cd", [P, 2, SQ], f32)
        b1s = at("b1s", [P, FC], f32)
        b2s = at("b2s", [P, E], f32)
        bps = at("bps", [P, E], f32)
        stats = at("stats", [P, TT, 6], f32)
        mv = at("mv", [P, TT, 2], f32)
        veps = at("veps", [P, TT], f32)
        mhalf = at("mhalf", [P, TT], f32)
        rstd = at("rstd", [P, TT], f32)
        negm = at("negm", [P, B, 2, 2, HP], f32)
        mm = at("mm", [2 * HP * 2, 2, 2, P], f32r)
        rc = at("rc", [P, 2, 2, 4], f32)

        SC = ctx.enter_context(nc.psum_tensor("SC", [P, 2, 2, 2, SQ], f32))
        G = ctx.enter_context(nc.psum_tensor("G", [P, 3, HALF], f32))
        T = ctx.enter_context(nc.psum_tensor("T", [P, HALF], f32))
        PV = G[:, 2, 0:SQ]

        x_in = [sem(f"x_in{b}") for b in range(B)]
        wqkv_in = [sem(f"wqkv_in{c}") for c in range(3)]
        w1_in, w2_in, wp_in, bias_in = (sem(n) for n in ("w1_in", "w2_in", "wp_in", "bias_in"))
        x_again = sem("x_again")
        stored = [sem(f"stored{u}") for u in range(TT)]
        ident_set, ident_ready, ones_ready, va_ones, mhalf_set = (
            sem(n) for n in ("ident_set", "ident_ready", "ones_ready", "va_ones", "mhalf_set"))
        wqkv_hi, wqkv_lo, w1_hi, w1_lo, w2_hi, w2_lo = (
            sem(n) for n in ("wqkv_hi", "wqkv_lo", "w1_hi", "w1_lo", "w2_hi", "w2_lo"))
        stats_done, mv_done, veps_done, rstd_done, xn_done = (
            sem(n) for n in ("stats_done", "mv_done", "veps_done", "rstd_done", "xn_done"))
        xt_made, xt_hi, xt_lo = sem("xt_made"), sem("xt_hi"), sem("xt_lo")
        qk_made, qk_hi, qk_lo = sem("qk_made"), sem("qk_hi"), sem("qk_lo")
        v_made, v_out, f1_made, gelu_done = sem("v_made"), sem("v_out"), sem("f1_made"), sem("gelu_done")
        h_hi, h_lo, warm_set = sem("h_hi"), sem("h_lo"), sem("warm_set")
        stacked = [sem(f"stacked{h}") for h in range(2)]
        ones_rows = sem("ones_rows")
        s_made, max_done, st_made, exp_done = sem("s_made"), sem("max_done"), sem("st_made"), sem("exp_done")
        mt_made, m_hi, m_lo = sem("mt_made"), sem("m_hi"), sem("m_lo")
        m_rows = [sem(f"m_rows{b}") for b in range(B)]
        pv_made, cd_out, ct_made, rc_done, norm_done = (
            sem(n) for n in ("pv_made", "cd_out", "ct_made", "rc_done", "norm_done"))
        bt_made, ct_hi, bt_out, wp_hi, wp_lo = (sem(n) for n in ("bt_made", "ct_hi", "bt_out", "wp_hi", "wp_lo"))
        f2_made, b2_half, yh_done, th_done, gate_done, bg_done, xb_done = (
            sem(n) for n in ("f2_made", "b2_half", "yh_done", "th_done", "gate_done", "bg_done", "xb_done"))
        pj_made, gated, fin_done = sem("pj_made"), sem("gated"), sem("fin_done")

        count = {}

        def nth(kind):
            count[kind] = count.get(kind, 0) + 1
            return count[kind]

        g_uses, g_free = [], []
        for s in order:
            if s[0] in ("QK", "V", "F1") or (s[0] == "F2" and s[1] < TT // 2 and s[2] == 0):
                g_uses.append(s)
                g_free.append(({"QK": qk_lo, "V": v_out, "F1": gelu_done, "F2": yh_done}[s[0]], nth("G" + s[0])))
        g_bank = {use: n % 3 for n, use in enumerate(g_uses)}

        def xt_bank(b, kc):
            return SC[:, b % 2, kc, 0, :]

        aside = {("CT", GROUPS - 1): 0, ("BT", 1, 3): 1}

        def late_bank(s):
            return 1 if s[0] == "BT" or s[:2] in (("F2", TT // 2 + 1), ("PJ", TT - 2)) else 0

        late_wait = {}
        last_read = [(gelu_done, 2 * FC), (gelu_done, 2 * FC)]
        for s in order:
            if s in aside:
                continue
            if s[0] == "BT" or (s[0] == "PJ" and s[2] == 0) or (s[0] == "F2" and s[1] >= TT // 2 and s[2] == 0):
                late_wait[s] = last_read[late_bank(s)]
                reader = {"F2": yh_done, "PJ": gated, "BT": bt_out}[s[0]]
                last_read[late_bank(s)] = (reader, KC * s[2] + s[1] + 1 if s[0] == "BT" else s[1] + 1)

        def f2_bank(u):
            return g_bank[("F2", u, 0)] if u < 4 else late_bank(("F2", u))

        sc_uses = steps("S", "ST")
        sc_free = [({"S": max_done, "ST": exp_done}[s[0]], s[1] + 1) for s in sc_uses]
        sc_slot = {s: n % 2 for n, s in enumerate(sc_uses)}
        t_uses = [s for s in steps("MT", "CT") if s not in aside]
        t_free = []
        for s in t_uses:
            t_free.append(({"MT": m_lo, "CT": norm_done}[s[0]], nth("T" + s[0])))

        def t_bank(s):
            if s in aside:
                return SC[:, 0, aside[s]].rearrange("p a c -> p (a c)")
            return G[:, late_bank(s)] if s[0] == "BT" else T

        def wait_free(eng, uses, free, use, ring):
            n = uses.index(use)
            if n >= ring:
                eng.wait_ge(*free[n - ring])

        block = ctx.enter_context(nc.Block())

        @block.sync
        def _(sp):
            x_t = x.rearrange("(b p t) e -> p b (t e)", p=P, t=2)
            out_t = out.rearrange("(b p t) e -> p b t e", p=P, t=2)
            for b in range(2):
                sp.dma_start(xs[:, 2 * b:2 * b + 2, :], x_t[:, b, :]).then_inc(x_in[b], 16)
            for c in range(3):
                sp.dma_start(wqkv_raw[:, c], wqkv[c]).then_inc(wqkv_in[c], 16)
            for b in range(2, B):
                sp.dma_start(xs[:, 2 * b:2 * b + 2, :], x_t[:, b, :]).then_inc(x_in[b], 16)
            sp.dma_start(w1_raw[:], w1).then_inc(w1_in, 16)
            sp.wait_ge(ones_ready, 1)
            for par in range(2):
                sp.dma_start(ks[64 * par + STK:64 * par + STM, :, :].bitcast(f32)
                             .rearrange("p h (b t) -> p (h b) t", t=SQ),
                             ones[0:2, None, :].to_broadcast([2, HP * B, SQ])).then_inc(ones_rows, 16)
            for h in range(2):
                cols = slice(h * HALF, (h + 1) * HALF)
                for i in range(4):
                    stack, parts = (qs, (0, 0, 1)) if i < 2 else (ks, (0, 1, 0))
                    sp.wait_ge(qk_hi, 4 * h + i + 1)
                    sp.wait_ge(qk_lo, 4 * h + i + 1)
                    for n, part in enumerate(parts):
                        row = 64 * (i % 2) + HN * n
                        sp.dma_start(stack[row:row + HN, :, cols].bitcast(f32),
                                     stage[:, h, i, part, :].bitcast(f32)).then_inc(stacked[h], 16)
                if h == 0:
                    sp.dma_start(w2_raw[:], w2).then_inc(w2_in, 16)
                    sp.dma_start(wps[:], wp).then_inc(wp_in, 16)
            for b in range(B):
                sp.wait_ge(m_hi, b + 1)
                sp.wait_ge(m_lo, b + 1)
                for qt in range(2):
                    for part in range(2):
                        c = b * SQ + qt * P
                        sp.dma_start(qs[STK + part:P:64, :, c:c + P].bitcast(f32),
                                     mm[qt * NH:(qt + 1) * NH, b % 2, part, :].bitcast(f32)).then_inc(m_rows[b], 16)
            sp.wait_ge(f1_made, 2 * FC)
            sp.dma_start(xb[:].rearrange("p (b t) e -> p b (t e)", t=2), x_t).then_inc(x_again, 16)
            for u in range(TT):
                sp.wait_ge(fin_done, u + 1)
                sp.dma_start(out_t[:, u // 2, u % 2, :],
                             fin[:, u % 4, :]).then_inc(stored[u], 16)
            for u in range(TT):
                sp.wait_ge(stored[u], 16)

        @block.gpsimd
        def _(pool):
            nc.gpsimd.memset(mhalf[:], -0.5).then_inc(mhalf_set, 1)
            nc.gpsimd.memset(ident[:], 0.0).then_inc(ident_set, 1)
            pool.wait_ge(ident_set, 1)
            nc.gpsimd.affine_select(out=ident[:], in_=ident[:], compare_op=ALU.not_equal, fill=1.0, base=0,
                                    pattern=[[-1, P]], channel_multiplier=1).then_inc(ident_ready, 1)
            nc.gpsimd.memset(ones[:], 1.0).then_inc(ones_ready, 1)
            nc.gpsimd.memset(VA[:, :, :, HN:VW], 1.0).then_inc(va_ones, 1)

            def rsqrt(b):
                pool.wait_ge(veps_done, b + 1)
                nc.gpsimd.tensor_tensor(rstd[:, 2 * b:2 * b + 2], veps[:, 2 * b:2 * b + 2],
                                        mhalf[:, 2 * b:2 * b + 2], ALU.pow).then_inc(rstd_done, 1)

            pool.wait_ge(mhalf_set, 1)
            rsqrt(0)
            rsqrt(1)
            for c in range(3):
                pool.wait_ge(wqkv_hi, c + 1)
                nc.gpsimd.tensor_tensor(wql[:, c], wqkv_raw[:, c], wqh[:, c].bitcast(f32),
                                        ALU.subtract).then_inc(wqkv_lo, 1)
            rsqrt(2)
            rsqrt(3)
            for kc in range(KC):
                pool.wait_ge(w1_hi, kc + 1)
                nc.gpsimd.tensor_tensor(w1l[:, kc, :], w1_raw[:, kc, :], w1h[:, kc, :].bitcast(f32),
                                        ALU.subtract).then_inc(w1_lo, 1)
            for q in range(2):
                pool.wait_ge(w2_hi, q + 1)
                fs = slice(4 * q, 4 * q + 4)
                nc.gpsimd.tensor_tensor(w2l[:, fs, :], w2_raw[:, fs, :], w2h[:, fs, :].bitcast(f32),
                                        ALU.subtract).then_inc(w2_lo, 1)
            for n in range(2 * FC):
                pool.wait_ge(h_hi, n + 1)
                nc.gpsimd.tensor_tensor(hTl[:, n % FC, :], hG[:, n % FC, :], hTh[:, n % FC, :].bitcast(f32),
                                        ALU.subtract).then_inc(h_lo, 1)
            pool.wait_ge(wp_hi, 1)
            nc.gpsimd.tensor_tensor(wpl[:], wps[:], wph[:].bitcast(f32), ALU.subtract).then_inc(wp_lo, 1)
            pool.wait_ge(x_again, 16)
            pool.wait_ge(bias_in, 48)
            for u in range(TT):
                pool.wait_ge(gate_done, u + 1)
                if u >= 2:
                    pool.wait_ge(xb_done, u - 1)
                nc.gpsimd.tensor_tensor(bg[:, u % 2, :], gate[:, u, :], bps[:], ALU.mult).then_inc(bg_done, 1)
                pool.wait_ge(bg_done, u + 1)
                nc.gpsimd.tensor_tensor(xb[:, u, :], xb[:, u, :], bg[:, u % 2, :], ALU.add).then_inc(xb_done, 1)

        @block.scalar
        def _(act):
            act.dma_start(b1s[:], b1).then_inc(bias_in, 16)
            act.dma_start(b2s[:], b2.to_broadcast([P, E])).then_inc(bias_in, 16)
            act.dma_start(bps[:], bp.to_broadcast([P, E])).then_inc(bias_in, 16)
            act.wait_ge(warm_set, 1)
            nc.scalar.activation(rc[0:1, 0, 0, 0:1], warm[0:1, 0:1], ACT.Gelu)

            def split_wqkv(c):
                act.wait_ge(wqkv_in[c], 16)
                nc.scalar.activation(wqh[:, c], wqkv_raw[:, c], ACT.Copy).then_inc(wqkv_hi, 1)

            split_wqkv(0)
            split_wqkv(1)
            n_qk = n_v = n_f1 = n_mt = n_bt = 0
            for s in order:
                if s[0] == "XT":
                    b = s[1]
                    act.wait_ge(xt_made, b + 1)
                    for kc in range(KC):
                        nc.scalar.activation(xTh[:, kc, b * SQ:(b + 1) * SQ], xt_bank(b, kc),
                                             ACT.Copy).then_inc(xt_hi, 1)
                    if b == 0:
                        split_wqkv(2)
                elif s[0] == "QK":
                    h, i = s[1:]
                    act.wait_ge(qk_made, n_qk + 1)
                    nc.scalar.activation(stage[:, h, i, 0, :], G[:, g_bank[s], :], ACT.Copy,
                                         scale=SCALE if i < 2 else 1.0).then_inc(qk_hi, 1)
                    n_qk += 1
                    if n_qk in (2, 3):
                        act.wait_ge(w1_in, 16)
                        kc = n_qk - 2
                        nc.scalar.activation(w1h[:, kc, :], w1_raw[:, kc, :], ACT.Copy).then_inc(w1_hi, 1)
                elif s[0] == "V":
                    h, p = s[1:]
                    act.wait_ge(v_made, n_v + 1)
                    tt = 4 * h + 2 * p
                    nc.scalar.activation(VA[:, tt:tt + 2, :, 0:HN],
                                         G[:, g_bank[s], :].rearrange("p (t n d) -> p t n d", t=2, d=HN),
                                         ACT.Copy).then_inc(v_out, 1)
                    n_v += 1
                    if n_v == 3:
                        act.wait_ge(w2_in, 16)
                        for q in range(2):
                            fs = slice(4 * q, 4 * q + 4)
                            nc.scalar.activation(w2h[:, fs, :], w2_raw[:, fs, :], ACT.Copy).then_inc(w2_hi, 1)
                elif s[0] == "F1":
                    f = s[1] % FC
                    if n_f1 == 0:
                        act.wait_ge(bias_in, 48)
                        act.wait_ge(xt_made, B)
                        act.wait_ge(wqkv_lo, 3)
                    if n_f1 == FC // 2:
                        act.wait_ge(w1_lo, 2)
                        act.wait_ge(w2_lo, 2)
                    if n_f1 == FC:
                        act.wait_ge(f2_made, TT // 2)
                    act.wait_ge(f1_made, n_f1 + 1)
                    nc.scalar.activation(hG[:, f, :], G[:, g_bank[s], :], ACT.Gelu,
                                         bias=b1s[:, f:f + 1]).then_inc(gelu_done, 1)
                    n_f1 += 1
                    act.wait_ge(gelu_done, n_f1)
                    nc.scalar.activation(hTh[:, f, :], hG[:, f, :], ACT.Copy).then_inc(h_hi, 1)
                elif s[0] == "MT":
                    if s[1] >= 2:
                        act.wait_ge(m_rows[s[1] - 2], 64)
                    act.wait_ge(mt_made, n_mt + 1)
                    nc.scalar.activation(mm[:, s[1] % 2, 0, :], T[0:2 * HP * 2, 0:P], ACT.Copy).then_inc(m_hi, 1)
                    n_mt += 1
                elif s[0] == "ST":
                    w = s[1]
                    act.wait_ge(st_made, w + 1)
                    if w < 4:
                        act.wait_ge(stacked[0], 192)
                    if w >= 4:
                        act.wait_ge(pv_made, (w - 4) // 2 + 1)
                    nc.scalar.activation(PT[:, w % 4], SC[:, sc_slot[s]], ACT.Exp).then_inc(exp_done, 1)
                    if w == 4:
                        act.wait_ge(wp_in, 16)
                        act.wait_ge(stacked[1], 192)
                        nc.scalar.activation(wph[:], wps[:], ACT.Copy).then_inc(wp_hi, 1)
                elif s[0] == "F2" and s[2] == 3:
                    u = s[1]
                    act.wait_ge(yh_done, u + 1)
                    if u >= 2:
                        act.wait_ge(gate_done, u - 1)
                    nc.scalar.activation(th[:, u % 2, :], yh[:, u % 2, :], ACT.Tanh).then_inc(th_done, 1)
                elif s[0] == "BT":
                    kc, j = s[1:]
                    act.wait_ge(bt_made, n_bt + 1)
                    if j >= 2:
                        act.wait_ge(pj_made, 2 * (j - 1))
                    nc.scalar.activation(cTh[:, j % 2, kc, :], t_bank(s)[:, 0:SQ], ACT.Copy).then_inc(ct_hi, 1)
                    n_bt += 1

        @block.vector
        def _(dve):
            def norm_stats(b):
                dve.wait_ge(x_in[b], 16)
                for t in (2 * b, 2 * b + 1):
                    nc.vector.bn_stats(stats[:, t, :], xs[:, t, :]).then_inc(stats_done, 1)
                for t in (2 * b, 2 * b + 1):
                    dve.wait_ge(stats_done, t + 1)
                    nc.vector.bn_aggr(mv[:, t, :], stats[:, t, :]).then_inc(mv_done, 1)
                dve.wait_ge(mv_done, 2 * b + 2)
                nc.vector.tensor_scalar_add(veps[:, 2 * b:2 * b + 2], mv[:, 2 * b:2 * b + 2, 1],
                                            EPS).then_inc(veps_done, 1)

            def norm_apply(b):
                dve.wait_ge(rstd_done, b + 1)
                for t in (2 * b, 2 * b + 1):
                    nc.vector.tensor_scalar(xs[:, t, :], xs[:, t, :], mv[:, t, 0:1], rstd[:, t:t + 1],
                                            ALU.subtract, ALU.mult).then_inc(xn_done, 1)

            def finish_gate(u):
                dve.wait_ge(yh_done, u + 1)
                dve.wait_ge(th_done, u + 1)
                nc.vector.scalar_tensor_tensor(gate[:, u, :], th[:, u % 2, :], 1.0, yh[:, u % 2, :],
                                               ALU.add, ALU.mult).then_inc(gate_done, 1)

            nc.vector.memset(warm[:], 0.0).then_inc(warm_set, 1)
            norm_stats(0)
            norm_stats(1)
            norm_apply(0)
            norm_apply(1)
            n_qk = n_mt = 0
            for s in order:
                if s[0] == "XT":
                    b = s[1]
                    cols = slice(b * SQ, (b + 1) * SQ)
                    for kc in range(KC):
                        dve.wait_ge(xt_hi, KC * b + kc + 1)
                        nc.vector.tensor_tensor(xTl[:, kc, cols], xt_bank(b, kc),
                                                xTh[:, kc, cols].bitcast(f32), ALU.subtract).then_inc(xt_lo, 1)
                    if b == 1:
                        norm_stats(2)
                        norm_stats(3)
                elif s[0] == "QK":
                    h, i = s[1:]
                    dve.wait_ge(qk_hi, n_qk + 1)
                    nc.vector.scalar_tensor_tensor(stage[:, h, i, 1, :], G[:, g_bank[s], :],
                                                   SCALE if i < 2 else 1.0, stage[:, h, i, 0, :].bitcast(f32),
                                                   ALU.mult, ALU.subtract).then_inc(qk_lo, 1)
                    n_qk += 1
                    if n_qk <= 2:
                        norm_apply(n_qk + 1)
                elif s[0] == "S":
                    b, hp = divmod(s[1], HP)
                    dve.wait_ge(s_made, s[1] + 1)
                    nc.vector.tensor_reduce(negm[:, b, :, :, hp].rearrange("p q a -> p a q"), SC[:, sc_slot[s]],
                                            axis=AX.X, op=ALU.max, negate=True).then_inc(max_done, 1)
                elif s[0] == "MT":
                    dve.wait_ge(m_hi, n_mt + 1)
                    nc.vector.tensor_tensor(mm[:, s[1] % 2, 1, :], T[0:2 * HP * 2, 0:P],
                                            mm[:, s[1] % 2, 0, :].bitcast(f32), ALU.subtract).then_inc(m_lo, 1)
                    n_mt += 1
                elif s[0] == "PV":
                    g = s[1]
                    dve.wait_ge(pv_made, g + 1)
                    if g >= 2:
                        dve.wait_ge(ct_made, g - 1)
                    nc.vector.tensor_copy(cd[:, g % 2, :], PV).then_inc(cd_out, 1)
                elif s[0] == "CT":
                    g = s[1]
                    j, b = divmod(g, B)
                    tv = t_bank(s)[:, 0:2 * P].rearrange("p (q m r) -> p q m r", q=2, r=32)
                    dve.wait_ge(ct_made, g + 1)
                    if g >= 2:
                        dve.wait_ge(norm_done, g - 1)
                    if g == 0:
                        dve.wait_ge(stacked[1], 192)
                    nc.vector.reciprocal(rc[:, g % 2], tv[:, :, :, HN]).then_inc(rc_done, 1)
                    dve.wait_ge(rc_done, g + 1)
                    if j >= 2 and b == 0:
                        dve.wait_ge(bt_made, 2 * (j - 1))
                    cols = slice(4 * HN * b, 4 * HN * (b + 1))
                    nc.vector.tensor_tensor(ctxn[:, j % 2, :, cols].rearrange("p q (m d) -> p q m d", d=HN),
                                            tv[:, :, :, 0:HN],
                                            rc[:, g % 2, :, :, None].to_broadcast([P, 2, 4, HN]),
                                            ALU.mult).then_inc(norm_done, 1)
                elif s[0] == "F2" and s[2] == 3:
                    u = s[1]
                    if u == 0:
                        dve.wait_ge(bias_in, 48)
                        nc.vector.tensor_scalar(b2s[:], b2s[:], 0.5, None, ALU.mult).then_inc(b2_half, 1)
                        dve.wait_ge(b2_half, 1)
                        dve.wait_ge(v_made, 4)
                    dve.wait_ge(f2_made, u + 1)
                    if u >= 2:
                        dve.wait_ge(gate_done, u - 1)
                    nc.vector.scalar_tensor_tensor(yh[:, u % 2, :], G[:, f2_bank(u), 0:E], 0.5, b2s[:],
                                                   ALU.mult, ALU.add).then_inc(yh_done, 1)
                    if u >= 1:
                        finish_gate(u - 1)
                elif s[0] == "GATE":
                    finish_gate(TT - 1)
                elif s[0] == "BT":
                    kc, j = s[1:]
                    dve.wait_ge(ct_hi, 2 * j + kc + 1)
                    nc.vector.tensor_tensor(cTl[:, j % 2, kc, :], t_bank(s)[:, 0:SQ],
                                            cTh[:, j % 2, kc, :].bitcast(f32), ALU.subtract).then_inc(bt_out, 1)
                elif s[0] == "PJ" and s[2] == KC - 1:
                    u = s[1]
                    dve.wait_ge(pj_made, u + 1)
                    dve.wait_ge(xb_done, u + 1)
                    if u >= 4:
                        dve.wait_ge(stored[u - 4], 16)
                    dst = fin[:, u % 4, :]
                    nc.vector.tensor_tensor(dst, G[:, late_bank(s), 0:E], gate[:, u, :], ALU.mult).then_inc(gated, 1)
                    dve.wait_ge(gated, u + 1)
                    nc.vector.tensor_tensor(dst, dst, xb[:, u, :], ALU.add).then_inc(fin_done, 1)

        @block.tensor
        def _(pe):
            def product(dst, lhs, rhs, chunks, first=True, last=True, rhs_hi=None, lhs_lo=None, rhs_lo=None,
                        passes=((0, 0), (1, 0), (0, 1))):
                todo = [(kc, a, b) for a, b in passes for kc in chunks]
                for n, (kc, a, b) in enumerate(todo):
                    if rhs_hi and (a, b) == (0, 0):
                        pe.wait_ge(rhs_hi[0], rhs_hi[1] + n + 1)
                    if rhs_lo and (a, b) == (0, 1):
                        pe.wait_ge(rhs_lo[0], rhs_lo[1] + n - 2 * len(chunks) + 1)
                    if lhs_lo and (a, b, kc) == (1, 0, chunks[0]):
                        pe.wait_ge(*lhs_lo)
                    m = nc.tensor.matmul(dst, lhs(kc, a), rhs(kc, b), start=first and n == 0,
                                         stop=last and n == len(todo) - 1)
                return m

            def wait_bank(s):
                if s in aside:
                    pe.wait_ge(exp_done, B * HP)
                elif s in late_wait:
                    pe.wait_ge(*late_wait[s])
                else:
                    wait_free(pe, t_uses, t_free, s, 1)

            def warm_up():
                for _ in range(WARM):
                    nc.tensor.matmul(T[:, 0:HALF // 2], warm[:, 0:P], warm[:], start=True, stop=True)

            pe.wait_ge(warm_set, 1)
            warm_up()
            pe.wait_ge(ident_ready, 1)
            for s in order:
                if s[0] == "XT":
                    b = s[1]
                    if b >= 2:
                        pe.wait_ge(xt_lo, KC * (b - 1))
                    for t in range(2):
                        pe.wait_ge(xn_done, 2 * b + t + 1)
                        for kc in range(KC):
                            last = nc.tensor.transpose(xt_bank(b, kc)[:, t * P:(t + 1) * P],
                                                       xs[:, 2 * b + t, kc * P:(kc + 1) * P], ident[:])
                    last.then_inc(xt_made, 1)
                elif s[0] == "QK":
                    h, i = s[1:]
                    pe.wait_ge(wqkv_hi, i // 2 + 1)
                    wait_free(pe, g_uses, g_free, s, 3)
                    cuts = [(0, SQ), (1, SQ)] if (h, i) == (0, 0) else [(h, HALF)]
                    for n, width in cuts:
                        cols = slice(n * width, (n + 1) * width)
                        seen = KC * (cols.stop // SQ - 1)
                        last = product(G[:, g_bank[s], n * width % HALF:n * width % HALF + width],
                                       lambda kc, a: (wqh, wql)[a][:, i // 2, kc, (i % 2) * P:(i % 2 + 1) * P],
                                       lambda kc, a: (xTh, xTl)[a][:, kc, cols], range(KC),
                                       rhs_hi=(xt_hi, seen), lhs_lo=(wqkv_lo, i // 2 + 1), rhs_lo=(xt_lo, seen))
                    last.then_inc(qk_made, 1)
                elif s[0] == "V":
                    h, p = s[1:]
                    pe.wait_ge(wqkv_lo, 3)
                    wait_free(pe, g_uses, g_free, s, 3)
                    for t in range(2):
                        c = (4 * h + 2 * p + t) * P
                        last = product(G[:, g_bank[s], t * E:(t + 1) * E],
                                       lambda kc, a: (xTh, xTl)[a][:, kc, c:c + P],
                                       lambda kc, a: (wqh, wql)[a][:, 2, kc, :], range(KC))
                    last.then_inc(v_made, 1)
                elif s[0] == "F1":
                    h, f = divmod(s[1], FC)
                    pe.wait_ge(w1_hi, 2)
                    wait_free(pe, g_uses, g_free, s, 3)
                    product(G[:, g_bank[s], :],
                            lambda kc, a: (w1h, w1l)[a][:, kc, f * P:(f + 1) * P],
                            lambda kc, a: (xTh, xTl)[a][:, kc, h * HALF:(h + 1) * HALF], range(KC),
                            lhs_lo=(w1_lo, 2)).then_inc(f1_made, 1)
                elif s[0] == "S":
                    b, hp = divmod(s[1], HP)
                    if hp == 0:
                        pe.wait_ge(stacked[b // 2], 192)
                    wait_free(pe, sc_uses, sc_free, s, 2)
                    for qt in range(2):
                        for par in range(2):
                            rows = slice(64 * par, 64 * par + STK)
                            c = b * SQ + qt * P
                            last = nc.tensor.matmul(SC[:, sc_slot[s], par, qt, :], qs[rows, hp, c:c + P],
                                                    ks[rows, hp, b * SQ:(b + 1) * SQ], start=True, stop=True)
                    last.then_inc(s_made, 1)
                elif s[0] == "MT":
                    b = s[1]
                    pe.wait_ge(max_done, HP * (b + 1))
                    wait_free(pe, t_uses, t_free, s, 1)
                    nc.tensor.transpose(T[0:2 * HP * 2, 0:P], negm[:, b].rearrange("p q a h -> p (q a h)"),
                                        ident[:]).then_inc(mt_made, 1)
                elif s[0] == "ST":
                    j, b = divmod(s[1] // 2, B)
                    hp = 2 * j + s[1] % 2
                    if hp == 0:
                        pe.wait_ge(m_rows[b], 64)
                        pe.wait_ge(ones_rows, 32)
                    wait_free(pe, sc_uses, sc_free, s, 2)
                    for kt in range(2):
                        for par in range(2):
                            rows = slice(64 * par, 64 * par + STM)
                            c = b * SQ + kt * P
                            last = nc.tensor.matmul(SC[:, sc_slot[s], par, kt, :], ks[rows, hp, c:c + P],
                                                    qs[rows, hp, b * SQ:(b + 1) * SQ], start=True, stop=True)
                    last.then_inc(st_made, 1)
                elif s[0] == "F2":
                    u, part = s[1:]
                    fs = range(2 * part, 2 * part + 2)
                    c = (u % 4) * P
                    pe.wait_ge(h_lo, FC * (u // 4) + fs[-1] + 1)
                    if part == 0:
                        pe.wait_ge(w2_lo, 2)
                        if u < 4:
                            wait_free(pe, g_uses, g_free, s, 3)
                        else:
                            wait_bank(s)
                    m = product(G[:, f2_bank(u), 0:E],
                                lambda fc, a: (hTh, hTl)[a][:, fc, c:c + P],
                                lambda fc, a: (w2h, w2l)[a][:, fc, :], fs, first=part == 0, last=part == 3)
                    if part == 3:
                        m.then_inc(f2_made, 1)
                elif s[0] == "PV":
                    g = s[1]
                    j, b = divmod(g, B)
                    pe.wait_ge(exp_done, 2 * g + 2)
                    if g == 0:
                        pe.wait_ge(v_out, 4)
                        pe.wait_ge(va_ones, 1)
                        pe.wait_ge(gelu_done, 2 * FC)
                    if g >= 1:
                        pe.wait_ge(cd_out, g)
                    for kt in range(2):
                        for m in range(4):
                            w = 2 * g + m // 2
                            last = nc.tensor.matmul(PV[32 * m:32 * m + VW, :], VA[:, 2 * b + kt, 4 * j + m, :],
                                                    PT[:, w % 4, m % 2, kt, :], start=(kt == 0), stop=(kt == 1))
                    last.then_inc(pv_made, 1)
                elif s[0] == "CT":
                    g = s[1]
                    pe.wait_ge(cd_out, g + 1)
                    wait_bank(s)
                    for qt in range(2):
                        cols = slice(qt * P, (qt + 1) * P)
                        last = nc.tensor.transpose(t_bank(s)[:, cols], cd[:, g % 2, cols], ident[:])
                    last.then_inc(ct_made, 1)
                elif s[0] == "BT":
                    kc, j = s[1:]
                    pe.wait_ge(norm_done, 4 * j + 2 * kc + 2)
                    wait_bank(s)
                    for qt in range(2):
                        last = nc.tensor.transpose(t_bank(s)[:, qt * P:(qt + 1) * P],
                                                   ctxn[:, j % 2, qt, kc * P:(kc + 1) * P], ident[:])
                    last.then_inc(bt_made, 1)
                elif s[0] == "PJ":
                    u, kc = s[1:]
                    j, qt = divmod(u, 2)
                    pe.wait_ge(ct_hi, KC * j + kc + 1)
                    if u == 0:
                        pe.wait_ge(wp_lo, 1)
                    if kc == 0:
                        wait_bank(s)
                    last = product(G[:, late_bank(s), 0:E],
                                   lambda k, a: (cTh, cTl)[a][:, j % 2, k, qt * P:(qt + 1) * P],
                                   lambda k, a: (wph, wpl)[a][:, k, :], range(kc, kc + 1),
                                   first=kc == 0, last=kc == KC - 1, lhs_lo=(bt_out, KC * j + kc + 1),
                                   passes=((0, 0), (0, 1), (1, 0)))
                    if kc == KC - 1:
                        last.then_inc(pj_made, 1)


def kernel(**inputs):
    import numpy as np
    import concourse.bacc as bacc
    from concourse.bass_utils import run_bass_kernel_spmd

    a = {n: np.asarray(v) for n, v in inputs.items()}
    x = a["L0_attn_query"].reshape(TOK, E)
    w = a["L0_attn_Wqkv"].reshape(2, 2, 4, 3, HN, E)
    qk = w[:, :, :, 0:2].transpose(3, 1, 4, 2, 0, 5).reshape(2 * E, E)
    v = w[:, :, :, 2].transpose(2, 0, 1, 3, 4).reshape(E, E)

    def chunks(wt):
        return np.ascontiguousarray(wt.reshape(-1, P, wt.shape[1]).transpose(1, 0, 2))

    arrays = {
        "x": x,
        "wqkv": np.stack([chunks(c.T) for c in (qk[:E], qk[E:], v)]),
        "w1": chunks(a["L0_ffn_proj1"].T),
        "b1": np.ascontiguousarray(a["L0_ffn_proj1_bias"].reshape(FC, P).T),
        "w2": chunks(a["L0_ffn_proj2"].T),
        "b2": a["L0_ffn_proj2_bias"].reshape(1, E),
        "wp": chunks(a["L0_attn_Wproj"].T),
        "bp": a["L0_attn_bproj"].reshape(1, E),
    }
    nc = bacc.Bacc("TRN2", target_bir_lowering=False, num_devices=1)
    f32 = mybir.dt.float32
    args = [nc.dram_tensor(n, v.shape, f32, kind="ExternalInput").ap() for n, v in arrays.items()]
    out = nc.dram_tensor("out", (TOK, E), f32, kind="ExternalOutput").ap()
    layer_kernel(nc, *args, out)
    r = run_bass_kernel_spmd(nc, [arrays], core_ids=[0])
    return r.results[0]["out"].reshape(B, SQ, E)
```
